# Optimizing a Trainium2 kernel written in Bass

```python
import numpy as np
import jax
import jax.numpy as jnp

def _softmax(x, axis=-1):
    return jax.nn.softmax(x, axis=axis)

def _gelu(x):
    return jax.nn.gelu(x, approximate=True)

def _silu(x):
    return jax.nn.silu(x)

def _sigmoid(x):
    return jax.nn.sigmoid(x)

def _layernorm(x, axis=-1, eps=1e-05):
    m = jnp.mean(x, axis=axis, keepdims=True)
    v = jnp.var(x, axis=axis, keepdims=True)
    return (x - m) / jnp.sqrt(v + eps)

def _scatter_add(tgt, idx, src, axis=0):
    return tgt.at[idx].add(src)

def _segment_sum(src, seg, n):
    return jax.ops.segment_sum(src, seg, n)
kernel_name = 'mk_decoder_postln_d1_seqx_r4_9ef18f'

def setup_inputs(seed: int=0):
    np.random.seed(seed)
    _w = jnp.asarray

    def _rec_inputs():
        import jax
        import jax.numpy as jnp
        _rk = jax.random.key(seed)
        x = 7.22e-05 + 1 * jax.random.normal(jax.random.fold_in(_rk, 1), (16, 128, 256), jnp.float32)
        _lenS = 128 - jax.random.randint(jax.random.fold_in(_rk, 7), (16,), 0, max(1, 128 // 4) + 1, jnp.int32)
        _lenS2 = 128 - jax.random.randint(jax.random.fold_in(_rk, 8), (16,), 0, max(1, 128 // 4) + 1, jnp.int32)
        _ctx_1024P = jax.random.normal(jax.random.fold_in(_rk, 11), (16, 16, 256), jnp.float32)
        _ctx_1024c = jax.random.dirichlet(jax.random.fold_in(_rk, 511), 0.3 * jnp.ones((16,), jnp.float32), (16, 128))
        _ctx_1024t = jnp.einsum('bsk,bkd->bsd', _ctx_1024c, _ctx_1024P)
        _ctx_1024t = _ctx_1024t * jax.lax.rsqrt(jnp.mean(jnp.square(_ctx_1024t)) + 1e-12) * 0.953939
        ctx_1024 = 4.13588e-05 + 0.999923 * (_ctx_1024t + 0.3 * jax.random.normal(jax.random.fold_in(_rk, 611), (16, 128, 256), jnp.float32))
        return (x, ctx_1024)
    x, ctx_1024 = _rec_inputs()

    def _L0_attn_setup():
        import jax, jax.numpy as jnp
        import numpy as np
        D_MODEL = 256
        N_HEADS = 16
        WINDOW = 64
        HEAD_DIM = D_MODEL // N_HEADS
        HALF = WINDOW // 2
        NWIN = WINDOW + 1
        LN_EPS = 1e-05

        def _layernorm(x, g, b):
            mu = jnp.mean(x, axis=-1, keepdims=True)
            var = jnp.var(x, axis=-1, keepdims=True)
            return (x - mu) * jax.lax.rsqrt(var + LN_EPS) * g + b

        def _linear_attention(q, k, v):
            q = jax.nn.elu(q) + 1.0
            k = jax.nn.elu(k) + 1.0
            kv = jnp.einsum('bsd,bse->bde', k, v)
            num = jnp.einsum('bsd,bde->bse', q, kv)
            denom = jnp.einsum('bsd,bd->bs', q, k.sum(axis=1))
            return num / (denom[..., None] + 1e-06)

        def _window_attention(q, k, v, rel_bias):
            B, S, _ = q.shape
            qh = q.reshape(B, S, N_HEADS, HEAD_DIM).transpose(0, 2, 1, 3)
            kh = k.reshape(B, S, N_HEADS, HEAD_DIM).transpose(0, 2, 1, 3)
            vh = v.reshape(B, S, N_HEADS, HEAD_DIM).transpose(0, 2, 1, 3)
            kp = jnp.pad(kh, ((0, 0), (0, 0), (HALF, HALF), (0, 0)))
            vp = jnp.pad(vh, ((0, 0), (0, 0), (HALF, HALF), (0, 0)))
            pos = jnp.arange(S)
            scale = np.float32(1.0 / np.sqrt(HEAD_DIM))

            def score_step(_, w):
                off = w - HALF
                ks = jax.lax.dynamic_slice_in_dim(kp, w, S, axis=2)
                s = jnp.einsum('bhsd,bhsd->bhs', qh, ks) * scale
                s = s + rel_bias[off + WINDOW][None, :, None]
                valid = (pos + off >= 0) & (pos + off < S)
                s = jnp.where(valid[None, None, :], s, -jnp.inf)
                return (None, s)
            _, scores = jax.lax.scan(score_step, None, jnp.arange(NWIN))
            attn = jax.nn.softmax(scores, axis=0)

            def out_step(acc, aw):
                a, w = aw
                vs = jax.lax.dynamic_slice_in_dim(vp, w, S, axis=2)
                return (acc + a[..., None] * vs, None)
            out, _ = jax.lax.scan(out_step, jnp.zeros_like(qh), (attn, jnp.arange(NWIN)))
            return out.transpose(0, 2, 1, 3).reshape(B, S, D_MODEL)
        key = jax.random.key(seed)
        ks = jax.random.split(key, 16)

        def lin(k, fan_in, shape):
            return (jax.random.normal(k, shape, jnp.float32) / np.sqrt(fan_in)).astype(jnp.float32)
        D = D_MODEL
        inp = {'x': jax.random.normal(ks[0], (2, 512, D), jnp.float32), 'wq_lin': lin(ks[1], D, (D, D)), 'bq_lin': jnp.zeros((D,), jnp.float32), 'wk_lin': lin(ks[2], D, (D, D)), 'bk_lin': jnp.zeros((D,), jnp.float32), 'wv_lin': lin(ks[3], D, (D, D)), 'bv_lin': jnp.zeros((D,), jnp.float32), 'wq_loc': lin(ks[4], D, (D, D)), 'bq_loc': jnp.zeros((D,), jnp.float32), 'wk_loc': lin(ks[5], D, (D, D)), 'bk_loc': jnp.zeros((D,), jnp.float32), 'wv_loc': lin(ks[6], D, (D, D)), 'bv_loc': jnp.zeros((D,), jnp.float32), 'wo': lin(ks[7], D, (D, D)), 'bo': jnp.zeros((D,), jnp.float32), 'wg1': lin(ks[8], 3 * D, (3 * D, D)), 'bg1': jnp.zeros((D,), jnp.float32), 'wg2': lin(ks[9], D, (D, D)), 'bg2': jnp.zeros((D,), jnp.float32), 'rel_bias': jax.random.normal(ks[10], (2 * WINDOW + 1, N_HEADS), jnp.float32), 'ln_g': jnp.ones((D,), jnp.float32), 'ln_b': jnp.zeros((D,), jnp.float32)}
        return inp
    _L0_attn_all = _L0_attn_setup()
    _L0_attn_in = {k: v for k, v in _L0_attn_all.items() if k in ('wq_lin', 'bq_lin', 'wk_lin', 'bk_lin', 'wv_lin', 'bv_lin', 'wq_loc', 'bq_loc', 'wk_loc', 'bk_loc', 'wv_loc', 'bv_loc', 'wo', 'bo', 'wg1', 'bg1', 'wg2', 'bg2', 'rel_bias', 'ln_g', 'ln_b')}
    del _L0_attn_all

    def _L0_xattn_setup():
        import jax, jax.numpy as jnp
        import numpy as np
        D_MODEL = 256
        N_HEADS = 16
        HEAD_DIM = D_MODEL // N_HEADS
        key = jax.random.key(seed)
        ks = jax.random.split(key, 7)
        B, S, D = (4, 512, D_MODEL)
        s = 1.0 / np.sqrt(D)
        return {'query': jax.random.normal(ks[0], (B, S, D), jnp.float32), 'key': jax.random.normal(ks[1], (B, S, D), jnp.float32), 'value': jax.random.normal(ks[2], (B, S, D), jnp.float32), 'Wq': jax.random.normal(ks[3], (D, D), jnp.float32) * s, 'Wk': jax.random.normal(ks[4], (D, D), jnp.float32) * s, 'Wv': jax.random.normal(ks[5], (D, D), jnp.float32) * s, 'Wo': jax.random.normal(ks[6], (D, D), jnp.float32) * s}
    _L0_xattn_all = _L0_xattn_setup()
    _L0_xattn_in = {k: v for k, v in _L0_xattn_all.items() if k in ('Wq', 'Wk', 'Wv', 'Wo')}
    del _L0_xattn_all

    def _L0_ffn_setup():
        import jax, jax.numpy as jnp
        import numpy as np
        from jax import lax
        B, S, H = (2, 256, 256)
        I = 128
        E = 32
        TOP_K = 4
        N_GROUP = 4
        TOPK_GROUP = 2
        SCALE = 2.5
        N_SHARED = 2
        SH_I = I * N_SHARED

        def _route(tokens, router_weight, router_bias):
            logits = tokens.astype(jnp.float32) @ router_weight.astype(jnp.float32).T
            scores = jax.nn.sigmoid(logits)
            sfc = scores + router_bias[None, :]
            T = tokens.shape[0]
            grp = sfc.reshape(T, N_GROUP, E // N_GROUP)
            group_scores = lax.top_k(grp, 2)[0].sum(-1)
            _, gidx = lax.top_k(group_scores, TOPK_GROUP)
            gmask = jax.nn.one_hot(gidx, N_GROUP, dtype=sfc.dtype).sum(1)
            smask = jnp.broadcast_to(gmask[:, :, None], (T, N_GROUP, E // N_GROUP)).reshape(T, E)
            tmp = jnp.where(smask > 0, sfc, 0.0)
            _, topk_idx = lax.top_k(tmp, TOP_K)
            topk_w = jnp.take_along_axis(scores, topk_idx, axis=1)
            topk_w = topk_w / (topk_w.sum(-1, keepdims=True) + 1e-20)
            topk_w = topk_w * SCALE
            return (topk_idx, topk_w)
        key = jax.random.key(seed)
        ks = jax.random.split(key, 10)
        std = 0.02
        return {'hidden_states': jax.random.normal(ks[0], (B, S, H), jnp.float32), 'router_weight': jax.random.normal(ks[1], (E, H), jnp.float32) * std, 'router_bias': jnp.zeros((E,), jnp.float32), 'gate_w': jax.random.normal(ks[2], (E, I, H), jnp.float32) * std, 'up_w': jax.random.normal(ks[3], (E, I, H), jnp.float32) * std, 'down_w': jax.random.normal(ks[4], (E, H, I), jnp.float32) * std, 'shared_gate_w': jax.random.normal(ks[5], (SH_I, H), jnp.float32) * std, 'shared_up_w': jax.random.normal(ks[6], (SH_I, H), jnp.float32) * std, 'shared_down_w': jax.random.normal(ks[7], (H, SH_I), jnp.float32) * std}
    _L0_ffn_all = _L0_ffn_setup()
    _L0_ffn_in = {k: v for k, v in _L0_ffn_all.items() if k in ('router_weight', 'router_bias', 'gate_w', 'up_w', 'down_w', 'shared_gate_w', 'shared_up_w', 'shared_down_w')}
    del _L0_ffn_all
    return {'x': x, 'ctx_1024': ctx_1024, 'L0_attn_wq_lin': _L0_attn_in['wq_lin'], 'L0_attn_bq_lin': _L0_attn_in['bq_lin'], 'L0_attn_wk_lin': _L0_attn_in['wk_lin'], 'L0_attn_bk_lin': _L0_attn_in['bk_lin'], 'L0_attn_wv_lin': _L0_attn_in['wv_lin'], 'L0_attn_bv_lin': _L0_attn_in['bv_lin'], 'L0_attn_wq_loc': _L0_attn_in['wq_loc'], 'L0_attn_bq_loc': _L0_attn_in['bq_loc'], 'L0_attn_wk_loc': _L0_attn_in['wk_loc'], 'L0_attn_bk_loc': _L0_attn_in['bk_loc'], 'L0_attn_wv_loc': _L0_attn_in['wv_loc'], 'L0_attn_bv_loc': _L0_attn_in['bv_loc'], 'L0_attn_wo': _L0_attn_in['wo'], 'L0_attn_bo': _L0_attn_in['bo'], 'L0_attn_wg1': _L0_attn_in['wg1'], 'L0_attn_bg1': _L0_attn_in['bg1'], 'L0_attn_wg2': _L0_attn_in['wg2'], 'L0_attn_bg2': _L0_attn_in['bg2'], 'L0_attn_rel_bias': _L0_attn_in['rel_bias'], 'L0_attn_ln_g': _L0_attn_in['ln_g'], 'L0_attn_ln_b': _L0_attn_in['ln_b'], 'L0_xattn_Wq': _L0_xattn_in['Wq'], 'L0_xattn_Wk': _L0_xattn_in['Wk'], 'L0_xattn_Wv': _L0_xattn_in['Wv'], 'L0_xattn_Wo': _L0_xattn_in['Wo'], 'L0_ffn_router_weight': _L0_ffn_in['router_weight'], 'L0_ffn_router_bias': _L0_ffn_in['router_bias'], 'L0_ffn_gate_w': _L0_ffn_in['gate_w'], 'L0_ffn_up_w': _L0_ffn_in['up_w'], 'L0_ffn_down_w': _L0_ffn_in['down_w'], 'L0_ffn_shared_gate_w': _L0_ffn_in['shared_gate_w'], 'L0_ffn_shared_up_w': _L0_ffn_in['shared_up_w'], 'L0_ffn_shared_down_w': _L0_ffn_in['shared_down_w']}

def reference(x, ctx_1024, L0_attn_wq_lin, L0_attn_bq_lin, L0_attn_wk_lin, L0_attn_bk_lin, L0_attn_wv_lin, L0_attn_bv_lin, L0_attn_wq_loc, L0_attn_bq_loc, L0_attn_wk_loc, L0_attn_bk_loc, L0_attn_wv_loc, L0_attn_bv_loc, L0_attn_wo, L0_attn_bo, L0_attn_wg1, L0_attn_bg1, L0_attn_wg2, L0_attn_bg2, L0_attn_rel_bias, L0_attn_ln_g, L0_attn_ln_b, L0_xattn_Wq, L0_xattn_Wk, L0_xattn_Wv, L0_xattn_Wo, L0_ffn_router_weight, L0_ffn_router_bias, L0_ffn_gate_w, L0_ffn_up_w, L0_ffn_down_w, L0_ffn_shared_gate_w, L0_ffn_shared_up_w, L0_ffn_shared_down_w):
    import jax
    import jax.numpy as jnp

    def _L0_attn_ref(x, wq_lin, bq_lin, wk_lin, bk_lin, wv_lin, bv_lin, wq_loc, bq_loc, wk_loc, bk_loc, wv_loc, bv_loc, wo, bo, wg1, bg1, wg2, bg2, rel_bias, ln_g, ln_b):
        import jax, jax.numpy as jnp
        import numpy as np
        D_MODEL = 256
        N_HEADS = 16
        WINDOW = 64
        HEAD_DIM = D_MODEL // N_HEADS
        HALF = WINDOW // 2
        NWIN = WINDOW + 1
        LN_EPS = 1e-05

        def _layernorm(x, g, b):
            mu = jnp.mean(x, axis=-1, keepdims=True)
            var = jnp.var(x, axis=-1, keepdims=True)
            return (x - mu) * jax.lax.rsqrt(var + LN_EPS) * g + b

        def _linear_attention(q, k, v):
            q = jax.nn.elu(q) + 1.0
            k = jax.nn.elu(k) + 1.0
            kv = jnp.einsum('bsd,bse->bde', k, v)
            num = jnp.einsum('bsd,bde->bse', q, kv)
            denom = jnp.einsum('bsd,bd->bs', q, k.sum(axis=1))
            return num / (denom[..., None] + 1e-06)

        def _window_attention(q, k, v, rel_bias):
            B, S, _ = q.shape
            qh = q.reshape(B, S, N_HEADS, HEAD_DIM).transpose(0, 2, 1, 3)
            kh = k.reshape(B, S, N_HEADS, HEAD_DIM).transpose(0, 2, 1, 3)
            vh = v.reshape(B, S, N_HEADS, HEAD_DIM).transpose(0, 2, 1, 3)
            kp = jnp.pad(kh, ((0, 0), (0, 0), (HALF, HALF), (0, 0)))
            vp = jnp.pad(vh, ((0, 0), (0, 0), (HALF, HALF), (0, 0)))
            pos = jnp.arange(S)
            scale = np.float32(1.0 / np.sqrt(HEAD_DIM))

            def score_step(_, w):
                off = w - HALF
                ks = jax.lax.dynamic_slice_in_dim(kp, w, S, axis=2)
                s = jnp.einsum('bhsd,bhsd->bhs', qh, ks) * scale
                s = s + rel_bias[off + WINDOW][None, :, None]
                valid = (pos + off >= 0) & (pos + off < S)
                s = jnp.where(valid[None, None, :], s, -jnp.inf)
                return (None, s)
            _, scores = jax.lax.scan(score_step, None, jnp.arange(NWIN))
            attn = jax.nn.softmax(scores, axis=0)

            def out_step(acc, aw):
                a, w = aw
                vs = jax.lax.dynamic_slice_in_dim(vp, w, S, axis=2)
                return (acc + a[..., None] * vs, None)
            out, _ = jax.lax.scan(out_step, jnp.zeros_like(qh), (attn, jnp.arange(NWIN)))
            return out.transpose(0, 2, 1, 3).reshape(B, S, D_MODEL)
        h = _layernorm(x, ln_g, ln_b)
        lin_out = _linear_attention(h @ wq_lin + bq_lin, h @ wk_lin + bk_lin, h @ wv_lin + bv_lin)
        win_out = _window_attention(h @ wq_loc + bq_loc, h @ wk_loc + bk_loc, h @ wv_loc + bv_loc, rel_bias)
        gate_in = jnp.concatenate([lin_out, win_out, h], axis=-1)
        gate = jax.nn.sigmoid(jnp.maximum(gate_in @ wg1 + bg1, 0.0) @ wg2 + bg2)
        out = gate * lin_out + (1.0 - gate) * win_out
        return out @ wo + bo + x

    def _L0_xattn_ref(query, key, value, Wq, Wk, Wv, Wo):
        import jax, jax.numpy as jnp
        import numpy as np
        D_MODEL = 256
        N_HEADS = 16
        HEAD_DIM = D_MODEL // N_HEADS
        B, S, D = query.shape
        H, Dh = (N_HEADS, HEAD_DIM)
        q = (query @ Wq.T).reshape(B, S, H, Dh).transpose(0, 2, 1, 3)
        k = (key @ Wk.T).reshape(B, S, H, Dh).transpose(0, 2, 1, 3)
        v = (value @ Wv.T).reshape(B, S, H, Dh).transpose(0, 2, 1, 3)
        scale = 1.0 / jnp.sqrt(jnp.asarray(Dh, q.dtype))
        scores = jnp.einsum('bhqd,bhkd->bhqk', q, k) * scale
        attn = jax.nn.softmax(scores, axis=-1)
        out = jnp.einsum('bhqk,bhkd->bhqd', attn, v)
        combined = out.transpose(0, 2, 1, 3).reshape(B, S, D)
        return combined @ Wo.T

    def _L0_ffn_ref(hidden_states, router_weight, router_bias, gate_w, up_w, down_w, shared_gate_w, shared_up_w, shared_down_w):
        import jax, jax.numpy as jnp
        import numpy as np
        from jax import lax
        B, S, H = (2, 256, 256)
        I = 128
        E = 32
        TOP_K = 4
        N_GROUP = 4
        TOPK_GROUP = 2
        SCALE = 2.5
        N_SHARED = 2
        SH_I = I * N_SHARED

        def _route(tokens, router_weight, router_bias):
            logits = tokens.astype(jnp.float32) @ router_weight.astype(jnp.float32).T
            scores = jax.nn.sigmoid(logits)
            sfc = scores + router_bias[None, :]
            T = tokens.shape[0]
            grp = sfc.reshape(T, N_GROUP, E // N_GROUP)
            group_scores = lax.top_k(grp, 2)[0].sum(-1)
            _, gidx = lax.top_k(group_scores, TOPK_GROUP)
            gmask = jax.nn.one_hot(gidx, N_GROUP, dtype=sfc.dtype).sum(1)
            smask = jnp.broadcast_to(gmask[:, :, None], (T, N_GROUP, E // N_GROUP)).reshape(T, E)
            tmp = jnp.where(smask > 0, sfc, 0.0)
            _, topk_idx = lax.top_k(tmp, TOP_K)
            topk_w = jnp.take_along_axis(scores, topk_idx, axis=1)
            topk_w = topk_w / (topk_w.sum(-1, keepdims=True) + 1e-20)
            topk_w = topk_w * SCALE
            return (topk_idx, topk_w)
        tokens = hidden_states.reshape(-1, H)
        topk_idx, topk_w = _route(tokens, router_weight, router_bias)
        gate_vals = jax.nn.silu(jnp.einsum('th,eih->tei', tokens, gate_w))
        up_vals = jnp.einsum('th,eih->tei', tokens, up_w)
        hidden_vals = gate_vals * up_vals
        expert_out = jnp.einsum('tei,ehi->teh', hidden_vals, down_w)
        sel = jnp.take_along_axis(expert_out, topk_idx[:, :, None], axis=1)
        mixed = (sel * topk_w[:, :, None].astype(sel.dtype)).sum(1)
        mixed = mixed.reshape(hidden_states.shape)
        sg = jax.nn.silu(jnp.einsum('bsh,ih->bsi', hidden_states, shared_gate_w))
        su = jnp.einsum('bsh,ih->bsi', hidden_states, shared_up_w)
        shared = jnp.einsum('bsi,hi->bsh', sg * su, shared_down_w)
        return mixed + shared
    x = _layernorm(x + _L0_attn_ref(x, L0_attn_wq_lin, L0_attn_bq_lin, L0_attn_wk_lin, L0_attn_bk_lin, L0_attn_wv_lin, L0_attn_bv_lin, L0_attn_wq_loc, L0_attn_bq_loc, L0_attn_wk_loc, L0_attn_bk_loc, L0_attn_wv_loc, L0_attn_bv_loc, L0_attn_wo, L0_attn_bo, L0_attn_wg1, L0_attn_bg1, L0_attn_wg2, L0_attn_bg2, L0_attn_rel_bias, L0_attn_ln_g, L0_attn_ln_b), axis=-1)
    x = _layernorm(x + _L0_xattn_ref(x, ctx_1024, ctx_1024, L0_xattn_Wq, L0_xattn_Wk, L0_xattn_Wv, L0_xattn_Wo), axis=-1)
    x = _layernorm(x + _L0_ffn_ref(x, L0_ffn_router_weight, L0_ffn_router_bias, L0_ffn_gate_w, L0_ffn_up_w, L0_ffn_down_w, L0_ffn_shared_gate_w, L0_ffn_shared_up_w, L0_ffn_shared_down_w), axis=-1)
    return x

_drawn_inputs = setup_inputs


def setup_inputs(seed=0):
    import zlib

    import numpy as np

    out = dict(_drawn_inputs(seed))
    spreads = {'L0_attn_bq_lin': (0.0, 0.8),
     'L0_attn_bk_lin': (0.0, 0.8),
     'L0_attn_bv_lin': (0.0, 0.355),
     'L0_attn_bq_loc': (0.0, 0.8),
     'L0_attn_bk_loc': (0.0, 0.8),
     'L0_attn_bv_loc': (0.0, 0.326),
     'L0_attn_bo': (0.0, 0.1),
     'L0_attn_bg1': (0.0, 0.8),
     'L0_attn_bg2': (0.0, 0.8),
     'L0_attn_ln_g': (1.0, 0.6),
     'L0_attn_ln_b': (0.0, 0.1),
     'L0_ffn_router_bias': (0.0, 0.502)}
    factors = {'L0_attn_wq_lin': 8.0,
     'L0_attn_wk_lin': 8.0,
     'L0_attn_wg1': 3.594,
     'L0_attn_wg2': 3.05,
     'L0_ffn_router_weight': 4.553,
     'L0_ffn_gate_w': 3.806,
     'L0_ffn_up_w': 3.773,
     'L0_ffn_down_w': 3.77,
     'L0_ffn_shared_gate_w': 3.386,
     'L0_ffn_shared_up_w': 3.346,
     'L0_ffn_shared_down_w': 3.332}
    for name, (base, spread) in spreads.items():
        noise = np.random.default_rng([zlib.crc32(name.encode()), seed]).standard_normal(out[name].shape)
        drawn = base * np.exp(spread * noise) if base else spread * noise
        out[name] = jnp.asarray(drawn.astype(out[name].dtype))
    for name, factor in factors.items():
        out[name] = (out[name] * factor).astype(out[name].dtype)
    return out
```

```python
from contextlib import ExitStack

import concourse.bass as bass
import numpy as np
from concourse import mybir

F32 = mybir.dt.float32
F16 = mybir.dt.float16
ALU = mybir.AluOpType
ACT = mybir.ActivationFunctionType
AX_X = mybir.AxisListType.X

U32 = mybir.dt.uint32

P = 128
D = 256
KT = D // P
NB = 16
NH = 16
HD = D // NH
HALF = 32
NG = 4
GH = NH // NG
LN_EPS = 1e-5
NE = 32
NGRP = 4
EG = NE // NGRP
TOPK = 4
EI = 128
EW = 6 * EI
ROUTE_SCALE = 2.5
NT = NB * TOPK + NE
NZ = 8
PAD = -3e38
TAKEN = 3e38
QK_SCALE = float(HD) ** -0.5
NEG = -1e30
TAB_STEPS, WEIGHT_STEPS, SUM_STEPS = 15, 12, 4

C_KVLIN, C_VLOC, C_QLIN, C_QLOC, C_KLOC = 0, 512, 768, 1024, 1280
C_WG1, C_WG2, C_WO = 1536, 2304, 2560
W1COLS = 2816
C_XQ, C_XK, C_XV, C_XO = 0, 256, 512, 768
C_SG, C_SU, C_SD = 1024, 1280, 1536
C_RT, W2COLS = 1792, 1824
WCHUNK = 256
WB = 4
NPROJ = C_WG1 // WCHUNK
W_PIECES = [(0, c, WCHUNK) for c in range(0, W1COLS, WCHUNK)] + [(1, c, 228) for c in range(0, W2COLS, 228)]
N1 = W1COLS // WCHUNK

V_G, V_B, V_BQLIN, V_BQLOC, V_BKLOC, V_BG1, V_BG2, NVEC = 0, 2, 4, 6, 8, 10, 12, 14


def group_heads(g):
    return [2 * g, 2 * g + 1, NH // 2 + 2 * g, NH // 2 + 2 * g + 1]


def wait(eng, sem, value):
    if not isinstance(value, int) or value > 0:
        eng.wait_ge(sem, value)


def pipeline(eng, lag, step, count=NB, unroll=2):
    first = -(-lag // unroll) + 1
    for i in range(first * unroll):
        step(i, i % unroll, i // unroll)
    with eng.Fori(first, count // unroll) as h:
        for slot in range(unroll):
            step(h * unroll + slot, slot, h)
    for i in range(count, count + lag):
        step(i, i % unroll, i // unroll)


def settle(eng, n, passed, sem, value):
    if not isinstance(n, int):
        eng.sem_inc(passed, 1)
        eng.wait_ge(sem, value)


def live(n, count=NB):
    return not isinstance(n, int) or 0 <= n < count


class Turns:

    def __init__(self, order, lags, reads, emptied):
        self.order, self.lags, self.reads, self.emptied = order, lags, reads, emptied

    def wait(self, pe, use, i):
        k = self.order.index(use)
        while True:
            k -= 3
            prev = self.order[k % len(self.order)]
            if prev is None:
                continue
            tile = i + k // len(self.order) - self.lags[prev]
            if not isinstance(tile, int) or 0 <= tile < NB:
                break
            if tile < -len(self.order):
                return
        pe.wait_ge(self.emptied[prev], self.reads.get(prev, 1) * (tile + 1))


def pieces_of_step(i):
    if i >= NB:
        each, k, lo, hi = -(-(len(W_PIECES) - N1) // 4), i - NB, N1, len(W_PIECES)
    else:
        each, k, lo, hi = -(-(N1 - NPROJ) // 2), i, NPROJ, N1
    return range(min(lo + k * each, hi), min(lo + (k + 1) * each, hi))


def at(n):
    return bass.ds(n, 1)


def decoder_kernel(nc, x, ctx_t, wcat, vecs, rowvecs, rel_bias, consts, masks, experts, rbias_d, out):
    es = ExitStack()
    with es:
        def sb(name, shape, dt=F32, st=es):
            return st.enter_context(nc.sbuf_tensor(name, shape, dt))

        stage_sems = []

        def sem(name):
            stage_sems.append(nc.alloc_semaphore(name=name))
            return stage_sems[-1]

        banks = [es.enter_context(nc.psum_tensor(f"bank{i}", [P, 512], F32)) for i in range(8)]
        xs = sb("xs", [P, NB, D])
        hT_hi = sb("hT_hi", [P, NB, KT, P], F16)
        hT_lo = sb("hT_lo", [P, NB, KT, P], F16)
        w2_hi = sb("w2_hi", [P, KT, W2COLS], F16)
        w2_lo = sb("w2_lo", [P, KT, W2COLS], F16)
        ident = sb("ident", [P, P])
        par = sb("par", [P, 2])
        vec = sb("vec", [P, NVEC])
        neghalf = sb("neghalf", [P, 1])

        x_in = [sem(f"x_in{c}") for c in range(4)]
        const_in = sem("const_in")
        rel_in = sem("rel_in")
        w_in = [sem(f"w_in{c}") for c in range(WB)]
        w_hi_done = sem("w_hi_done")
        w_lo_done = sem("w_lo_done")
        setup = sem("setup")
        halfbg_ready = sem("halfbg_ready")
        zero_set, zeroed = sem("zero_set"), sem("zeroed")
        dve_passed, pool_passed = sem("dve_passed"), sem("pool_passed")

        x_rows = nc.dram_tensor("x_rows", (NT * P, 2 * D), F16, kind="Internal").ap()
        y_rows = nc.dram_tensor("y_rows", (NT * P, D), F32, kind="Internal").ap()
        x_tiles = x.rearrange("b p d -> p b d")
        w_tiles = wcat.rearrange("(k p) c -> p k c", p=P)

        lasting = len(stage_sems)
        with ExitStack() as st:
            def s1(name, shape, dt=F32):
                return sb(name, shape, dt, st)

            w_hi = s1("w_hi", [P, KT, W1COLS], F16)
            w_lo = s1("w_lo", [P, KT, W1COLS], F16)
            w_parts = ((w_hi, w2_hi), (w_lo, w2_lo))
            wst = s1("wst", [P, WB, KT, WCHUNK])
            rel = s1("rel", [P, NG, GH, P])
            zeros = s1("zeros", [P, 2 * D], F16)
            rows = s1("rows", [P, 4 * D])
            stats = s1("stats", [P, 2, 6])
            mv = s1("mv", [P, 2, 2])
            vareps = s1("vareps", [P, 2, 1])
            rstd = s1("rstd", [P, 2, 1])
            xn = s1("xn", [P, 2, D])
            hTf = s1("hTf", [P, 2, KT, P])
            kq = s1("kq", [P, 2, 2 * D])
            kq_neg = s1("kq_neg", [P, 2, 2 * D])
            kq_exp = s1("kq_exp", [P, 2, 2 * D])
            vlin = s1("vlin", [P, 2, D + 1])
            vloc = s1("vloc", [P, 2, NH, HD + 1])
            qkf = s1("qkf", [P, 2, 2, KT, P])
            q_hi = s1("q_hi", [P, 2, KT, P], F16)
            q_lo = s1("q_lo", [P, 2, KT, P], F16)
            k_hi = s1("k_hi", [P, 2, KT, 2, P], F16)
            k_lo = s1("k_lo", [P, 2, KT, 2, P], F16)
            sc = s1("sc", [P, NG, GH, P])
            mx = s1("mx", [P, 2, NG, GH])
            pT = s1("pT", [P, 2, GH, P])
            rsum = s1("rsum", [P, 2, NH])
            kvs = s1("kvs", [P, 2, KT, D + 1])
            den = s1("den", [P, 2, 1])
            rden = s1("rden", [P, 2, 1])
            lw = s1("lw", [P, 2, 2, D])
            lwTf = s1("lwTf", [P, 2, 4, P])
            lwT_hi = s1("lwT_hi", [P, 2, 4, P], F16)
            lwT_lo = s1("lwT_lo", [P, 2, 4, P], F16)
            lsum = s1("lsum", [P, 2, KT, P])
            ldif = s1("ldif", [P, 2, KT, P])
            z1f = s1("z1f", [P, 2, KT, P])
            z1_hi = s1("z1_hi", [P, 2, KT, P], F16)
            z1_lo = s1("z1_lo", [P, 2, KT, P], F16)
            gt = s1("gt", [P, 2, KT, P])
            mix = s1("mix", [P, 2, KT, P])
            mix_hi = s1("mix_hi", [P, 2, KT, P], F16)
            mix_lo = s1("mix_lo", [P, 2, KT, P], F16)
            xb = s1("xb", [P, 2, D])
            yt = s1("yt", [P, 2, D])
            vareps2 = s1("vareps2", [P, 2, 1])
            rstd2 = s1("rstd2", [P, 2, 1])
            stats2 = s1("stats2", [P, 2, 6])
            mv2 = s1("mv2", [P, 2, 2])
            halfbg2 = s1("halfbg2", [P, KT])

            sc_bank, pT_bank, o_bank, turn = banks[0:2], banks[2:4], banks[4], banks[5:8]
            TURNS = ["T", "KV0", "KV1", "Z2", "PJ1", "PJ2", "T2", "PJ3", "PJ4", "PJ5", "Z1", "WO", "NUM"]
            ORDER = TURNS + [None, None]
            LAGS = {"T": 1, "PJ1": 1, "PJ2": 1, "PJ3": 1, "PJ4": 1, "PJ5": 1, "KV0": 2, "KV1": 2, "NUM": 2,
                    "T2": 3, "Z1": 3, "Z2": 4, "WO": 4}
            bank_of = {u: turn[ORDER.index(u) % 3] for u in TURNS}
            filled = {u: sem(f"ps_{u}") for u in TURNS}
            emptied = {u: sem(f"rd_{u}") for u in TURNS}

            turns = Turns(ORDER, LAGS, {"Z1": 2, "Z2": 2, "PJ4": 2, "PJ5": 2, "T2": 1}, emptied)
            wait_turn = turns.wait

            ln_stat, ln_mv, ln_var, ln_rstd = sem("ln_stat"), sem("ln_mv"), sem("ln_var"), sem("ln_rstd")
            xn_ready = sem("xn_ready")
            hTf_ready, hThi_ready, hTlo_ready = sem("hTf_ready"), sem("hThi_ready"), sem("hTlo_ready")
            kq_min, kq_ex, kq_ready = sem("kq_min"), sem("kq_ex"), sem("kq_ready")
            qhi_r, qlo_r = sem("qhi_r"), sem("qlo_r")
            khi_r, klo_r = sem("khi_r"), sem("klo_r")
            sc_ps, sc_rd, sc_sub, sc_exp = sem("sc_ps"), sem("sc_rd"), sem("sc_sub"), sem("sc_exp")
            pT_ps, pT_rd = sem("pT_ps"), sem("pT_rd")
            pv_ps, pv_rec, pv_rd = sem("pv_ps"), sem("pv_rec"), sem("pv_rd")
            den_r, rden_r = sem("den_r"), sem("rden_r")
            lwhi_r, lwlo_r = sem("lwhi_r"), sem("lwlo_r")
            lsum_r, ldif_r = sem("lsum_r"), sem("ldif_r")
            z1hi_r, z1lo_r = sem("z1hi_r"), sem("z1lo_r")
            mixa, mixb, mixhi_r, mixlo_r = sem("mixa"), sem("mixb"), sem("mixhi_r"), sem("mixlo_r")
            xb_r = sem("xb_r")
            ln2_stat, ln2_mv, ln2_var, ln2_rstd = sem("ln2_stat"), sem("ln2_mv"), sem("ln2_var"), sem("ln2_rstd")
            x1_ready = sem("x1_ready")
            sc_part = sem("sc_part")
            kv_half = sem("kv_half")
            LAG = 5

            with nc.Block() as block:
                @block.sync
                def _(sp):
                    sp.dma_start(xs[:, 0:4, :], x_tiles[:, 0:4, :]).then_inc(x_in[0], 16)
                    sp.dma_start(ident[:], consts[:, 0:P]).then_inc(const_in, 16)
                    sp.dma_start(vec[:], vecs).then_inc(const_in, 16)
                    sp.dma_start(par[:], masks).then_inc(const_in, 16)
                    sp.dma_start(rows[:], rowvecs.rearrange("(a n) -> a n", a=1).broadcast_to([P, 4 * D])
                                 ).then_inc(const_in, 16)
                    for c, (t, col, width) in enumerate(W_PIECES):
                        wait(sp, w_lo_done, c - WB + 1)
                        sp.dma_start(wst[:, c % WB, :, 0:width], w_tiles[:, :, t * W1COLS + col:t * W1COLS + col + width]).then_inc(w_in[c % WB], 16)
                        if c == N1:
                            sp.wait_ge(zero_set, 1)
                            for k in range(NZ):
                                sp.dma_start(x_rows.rearrange("(z a p) d -> z p a d", p=P, z=NZ)[k],
                                             zeros[:].unsqueeze(1).to_broadcast([P, NT // NZ, 2 * D])).then_inc(zeroed, 16)
                        if c == 3:
                            sp.dma_start(rel[:].rearrange("p g h k -> p (g h k)"), rel_bias).then_inc(rel_in, 16)
                        if c in (1, 2, 5):
                            k = {1: 1, 2: 2, 5: 3}[c]
                            sp.dma_start(xs[:, 4 * k:4 * k + 4, :], x_tiles[:, 4 * k:4 * k + 4, :]).then_inc(x_in[k], 16)

                @block.gpsimd
                def _(pool):
                    pool.memset(zeros[:], 0.0).then_inc(zero_set, 1)
                    pool.memset(neghalf[:], -0.5).then_inc(setup, 1)
                    pool.memset(vlin[:, :, D:D + 1], 1.0).then_inc(setup, 1)
                    pool.memset(vloc[:, :, :, HD:HD + 1], 1.0).then_inc(setup, 1)
                    pool.wait_ge(setup, 3)

                    def step(i, p, h):
                        n = i
                        if live(n):
                            wait(pool, ln_var, n + 1)
                            wait(pool, xn_ready, n - 1)
                            pool.tensor_tensor(rstd[:, p], vareps[:, p], neghalf[:], ALU.pow).then_inc(ln_rstd, 1)
                        def subtract_max(g):
                            n, q = i - 2, p
                            if live(n):
                                wait(pool, sc_rd, NG * n + g + 1)
                                wait(pool, sc_part, (GH - 1) * (NG * n + g + 1))
                                pool.tensor_tensor(sc[:, g], sc[:, g], mx[:, q, g].unsqueeze(2).to_broadcast([P, GH, P]),
                                                   ALU.subtract).then_inc(sc_sub, 1)

                        subtract_max(0)
                        n, q = i - 5, 1 - p
                        if live(n):
                            wait(pool, ln2_var, n + 1)
                            wait(pool, x1_ready, n - 1)
                            pool.tensor_tensor(rstd2[:, q], vareps2[:, q], neghalf[:], ALU.pow).then_inc(ln2_rstd, 1)
                        subtract_max(1)
                        subtract_max(2)
                        n, q = i - 3, 1 - p
                        if live(n):
                            wait(pool, emptied["T2"], n + 1)
                            wait(pool, mixb, n - 1)
                            pool.tensor_tensor(lsum[:, q], lwTf[:, q, 0:2], lwTf[:, q, 2:4], ALU.add).then_inc(lsum_r, 1)
                            pool.tensor_tensor(ldif[:, q], lwTf[:, q, 0:2], lwTf[:, q, 2:4], ALU.subtract).then_inc(ldif_r, 1)
                        subtract_max(3)
                        n, q = i - 1, 1 - p
                        if live(n):
                            wait(pool, kv_half, 2 * (n + 1))
                            wait(pool, emptied["PJ3"], n + 1)
                            wait(pool, kq_ex, n - 1)
                            settle(pool, n, pool_passed, setup, 3)
                            pool.tensor_scalar(kq_neg[:, q], kq[:, q], 0.0, None, ALU.min).then_inc(kq_min, 1)

                    pipeline(pool, LAG, step)

                @block.scalar
                def _(act):
                    def high_part(c):
                        t, col, width = W_PIECES[c]
                        act.wait_ge(w_in[c % WB], 16 * (c // WB + 1))
                        act.activation(w_parts[0][t][:, :, col:col + width], wst[:, c % WB, :, 0:width], ACT.Copy).then_inc(w_hi_done, 1)

                    for c in range(NPROJ):
                        high_part(c)
                    act.wait_ge(const_in, 64)
                    act.wait_ge(halfbg_ready, 1)

                    def step(i, p, h):
                        def qk_evac():
                            n, q = i - 1, 1 - p
                            if live(n):
                                for s, (u, v) in enumerate((("PJ4", V_BQLOC), ("PJ5", V_BKLOC))):
                                    act.wait_ge(filled[u], n + 1)
                                    wait(act, klo_r if s else qlo_r, (n - 1) * (2 if s else 1))
                                    for k in range(KT):
                                        act.activation(qkf[:, q, s, k], bank_of[u][:, k * P:(k + 1) * P], ACT.Identity,
                                                       bias=vec[:, v + k:v + k + 1]).then_inc(emptied[u], 1)

                        def exps(g):
                            n, q = i - 2, p
                            if live(n):
                                act.wait_ge(sc_sub, NG * n + g + 1)
                                act.activation(sc[:, g], sc[:, g], ACT.Exp).then_inc(sc_exp, 1)

                        def pT_evac(g):
                            n = i - 2 if g < NG // 2 else i - 3
                            if live(n):
                                act.wait_ge(pT_ps, NG * n + g + 1)
                                wait(act, pv_ps, NG * n + g - 1)
                                act.activation(pT[:, g % 2], pT_bank[g % 2][:].rearrange("p (h k) -> p h k", h=GH), ACT.Copy
                                               ).then_inc(pT_rd, 1)

                        pT_evac(2)
                        n, q = i - 1, 1 - p
                        if live(n):
                            act.wait_ge(filled["T"], n + 1)
                            wait(act, hTlo_ready, n - 1)
                            for k in range(KT):
                                act.activation(hTf[:, q, k], bank_of["T"][:, k * P:(k + 1) * P], ACT.Identity,
                                               bias=vec[:, V_B + k:V_B + k + 1], scale=vec[:, V_G + k:V_G + k + 1]
                                               ).then_inc(emptied["T"] if k else hTf_ready, 1)
                            act.wait_ge(emptied["T"], n + 1)
                            act.wait_ge(hTf_ready, n + 1)
                            act.activation(hT_hi[:, at(n)].rearrange("p a k t -> p (a k t)"), hTf[:, q].rearrange("p k t -> p (k t)"), ACT.Copy).then_inc(hThi_ready, 1)
                        pT_evac(3)
                        n, q = i - 2, p
                        if live(n):
                            for k in range(KT):
                                act.wait_ge(filled[f"KV{k}"], n + 1)
                                wait(act, filled["NUM"], n - 1)
                                act.activation(kvs[:, q, k], bank_of[f"KV{k}"][:, 0:D + 1], ACT.Copy).then_inc(emptied[f"KV{k}"], 1)
                        exps(0)
                        n, q = i - 4, p
                        if live(n):
                            act.wait_ge(filled["Z2"], n + 1)
                            wait(act, mixa, n - 1)
                            for k in range(KT):
                                act.activation(gt[:, q, k], bank_of["Z2"][:, k * P:(k + 1) * P], ACT.Tanh,
                                               bias=halfbg2[:, k:k + 1], scale=0.5).then_inc(emptied["Z2"], 1)
                        exps(1)
                        exps(2)
                        pT_evac(0)
                        n, q = i - 3, 1 - p
                        if live(n):
                            act.wait_ge(filled["T2"], n + 1)
                            wait(act, lwlo_r, n - 1)
                            wait(act, ldif_r, n - 1)
                            act.activation(lwTf[:, q], bank_of["T2"][:].rearrange("p (h k) -> p h k", h=4), ACT.Copy).then_inc(emptied["T2"], 1)
                            act.wait_ge(emptied["T2"], n + 1)
                            wait(act, emptied["Z1"], 2 * (n - 1))
                            act.activation(lwT_hi[:, q], lwTf[:, q], ACT.Copy).then_inc(lwhi_r, 1)
                        n, q = i - 4, p
                        if live(n):
                            act.wait_ge(mixb, n + 1)
                            wait(act, filled["WO"], n - 1)
                            act.activation(mix_hi[:, q], mix[:, q], ACT.Copy).then_inc(mixhi_r, 1)
                        exps(3)
                        pT_evac(1)
                        n, q = i - 1, 1 - p
                        if live(n):
                            act.wait_ge(kq_min, n + 1)
                            wait(act, kq_ready, n - 1)
                            act.activation(kq_exp[:, q], kq_neg[:, q], ACT.Exp).then_inc(kq_ex, 1)
                        qk_evac()
                        n, q = i - 3, 1 - p
                        if live(n):
                            act.wait_ge(filled["Z1"], n + 1)
                            wait(act, z1lo_r, n - 1)
                            for k in range(KT):
                                act.activation(z1f[:, q, k], bank_of["Z1"][:, k * P:(k + 1) * P], ACT.Relu,
                                               bias=vec[:, V_BG1 + k:V_BG1 + k + 1]).then_inc(emptied["Z1"], 1)
                            act.wait_ge(emptied["Z1"], 2 * (n + 1))
                            wait(act, filled["Z2"], n - 1)
                            act.activation(z1_hi[:, q], z1f[:, q], ACT.Copy).then_inc(z1hi_r, 1)
                        if isinstance(i, int):
                            for c in pieces_of_step(i):
                                high_part(c)

                    pipeline(act, LAG, step)

                @block.vector
                def _(dve):
                    def low_part(c):
                        t, col, width = W_PIECES[c]
                        dve.wait_ge(w_hi_done, c + 1)
                        cs = slice(col, col + width)
                        dve.tensor_tensor(w_parts[1][t][:, :, cs], wst[:, c % WB, :, 0:width], w_parts[0][t][:, :, cs], ALU.subtract
                                          ).then_inc(w_lo_done, 1)

                    for c in range(NPROJ):
                        low_part(c)
                    dve.wait_ge(const_in, 64)
                    dve.tensor_scalar(halfbg2[:], vec[:, V_BG2:V_BG2 + 2], 0.5, None, ALU.mult).then_inc(halfbg_ready, 1)
                    dve.wait_ge(rel_in, 16)
                    for c in range(4):
                        dve.wait_ge(x_in[c], 16)

                    def step(i, p, h):
                        n = i
                        if live(n):
                            xt = xs[:, at(n)].rearrange("p a d -> p (a d)")
                            wait(dve, ln_mv, n - 1)
                            dve.bn_stats(stats[:, p], xt).then_inc(ln_stat, 1)
                            dve.wait_ge(ln_stat, n + 1)
                            wait(dve, xn_ready, n - 1)
                            settle(dve, n, dve_passed, const_in, 64)
                            dve.bn_aggr(mv[:, p], stats[:, p]).then_inc(ln_mv, 1)
                            dve.wait_ge(ln_mv, n + 1)
                            wait(dve, ln_rstd, n - 1)
                            dve.tensor_scalar(vareps[:, p], mv[:, p, 1:2], LN_EPS, None, ALU.add).then_inc(ln_var, 1)
                        def maxes(g):
                            n, q = i - 2, p
                            if live(n):
                                dve.wait_ge(sc_ps, NG * n + g + 1)
                                wait(dve, pT_ps, NG * (n - 1) + g + 1)
                                wait(dve, sc_sub, NG * (n - 2) + g + 1)
                                settle(dve, n, dve_passed, const_in, 64)
                                for j in range(GH):
                                    dve.tensor_tensor_reduce(
                                        out=sc[:, g, j], in0=sc_bank[g % 2][:, j * P:(j + 1) * P], in1=rel[:, g, j],
                                        scale=1.0, scalar=NEG, op0=ALU.add, op1=ALU.max, accum_out=mx[:, q, g, j:j + 1]
                                    ).then_inc(sc_rd if j == GH - 1 else sc_part, 1)

                        maxes(0)
                        n, q = i - 5, 1 - p
                        if live(n):
                            xt = xs[:, at(n)].rearrange("p a d -> p (a d)")
                            wait(dve, emptied["WO"], n - 1)
                            dve.scalar_tensor_tensor(xb[:, q], xt, 2.0, rows[:, 3 * D:4 * D], ALU.mult, ALU.add).then_inc(xb_r, 1)
                            dve.wait_ge(xb_r, n + 1)
                            dve.wait_ge(filled["WO"], n + 1)
                            wait(dve, x1_ready, n - 1)
                            dve.scalar_tensor_tensor(yt[:, q], bank_of["WO"][:, 0:D], 0.5, xb[:, q], ALU.mult, ALU.add).then_inc(emptied["WO"], 1)
                            dve.wait_ge(emptied["WO"], n + 1)
                            wait(dve, ln2_mv, n - 1)
                            dve.bn_stats(stats2[:, q], yt[:, q]).then_inc(ln2_stat, 1)
                            dve.wait_ge(ln2_stat, n + 1)
                            wait(dve, x1_ready, n - 1)
                            settle(dve, n, dve_passed, const_in, 64)
                            dve.bn_aggr(mv2[:, q], stats2[:, q]).then_inc(ln2_mv, 1)
                            dve.wait_ge(ln2_mv, n + 1)
                            wait(dve, ln2_rstd, n - 1)
                            dve.tensor_scalar(vareps2[:, q], mv2[:, q, 1:2], LN_EPS, None, ALU.add).then_inc(ln2_var, 1)
                        n, q = i - 1, 1 - p
                        if live(n):
                            dve.wait_ge(hThi_ready, n + 1)
                            dve.tensor_tensor(hT_lo[:, at(n)].rearrange("p a k t -> p (a k t)"), hTf[:, q].rearrange("p k t -> p (k t)"),
                                              hT_hi[:, at(n)].rearrange("p a k t -> p (a k t)"), ALU.subtract).then_inc(hTlo_ready, 1)
                        maxes(1)
                        n = i
                        if live(n):
                            xt = xs[:, at(n)].rearrange("p a d -> p (a d)")
                            dve.wait_ge(ln_rstd, n + 1)
                            wait(dve, filled["T"], n - 1)
                            dve.tensor_scalar(xn[:, p], xt, mv[:, p, 0:1], rstd[:, p], ALU.subtract, ALU.mult).then_inc(xn_ready, 1)
                        n, q = i - 3, 1 - p
                        if live(n):
                            heads = o_bank[:, 0:NH * (HD + 1)].rearrange("p (h d) -> p h d", h=NH)
                            dve.wait_ge(pv_ps, NG * (n + 1))
                            wait(dve, pv_rd, n - 1)
                            dve.reciprocal(rsum[:, q], heads[:, :, HD]).then_inc(pv_rec, 1)
                            dve.wait_ge(pv_rec, n + 1)
                            wait(dve, filled["T2"], n - 1)
                            dve.tensor_tensor(lw[:, q, 1].rearrange("p (h d) -> p h d", h=NH), heads[:, :, 0:HD],
                                              rsum[:, q].unsqueeze(2).to_broadcast([P, NH, HD]), ALU.mult).then_inc(pv_rd, 1)
                        n, q = i - 5, 1 - p
                        if live(n):
                            dve.wait_ge(ln2_rstd, n + 1)
                            dve.tensor_scalar(xs[:, at(n)].rearrange("p a d -> p (a d)"), yt[:, q], mv2[:, q, 0:1], rstd2[:, q],
                                              ALU.subtract, ALU.mult).then_inc(x1_ready, 1)
                        n, q = i - 1, 1 - p
                        if live(n):
                            dve.wait_ge(filled["PJ1"], n + 1)
                            wait(dve, kq_ready, n - 1)
                            wait(dve, kq_min, n - 1)
                            dve.tensor_tensor(kq[:, q, 0:D], bank_of["PJ1"][:, 0:D], rows[:, 0:D], ALU.add).then_inc(kv_half, 1)
                            wait(dve, filled["KV1"], n - 1)
                            dve.tensor_tensor(vlin[:, q, 0:D], bank_of["PJ1"][:, D:2 * D], rows[:, D:2 * D], ALU.add).then_inc(emptied["PJ1"], 1)
                        maxes(2)
                        n, q = i - 4, p
                        if live(n):
                            dve.wait_ge(emptied["Z2"], 2 * (n + 1))
                            dve.wait_ge(ldif_r, n + 1)
                            wait(dve, mixlo_r, n - 1)
                            dve.tensor_tensor(gt[:, q], gt[:, q], ldif[:, q], ALU.mult).then_inc(mixa, 1)
                            dve.wait_ge(mixa, n + 1)
                            dve.wait_ge(lsum_r, n + 1)
                            dve.tensor_tensor(mix[:, q], gt[:, q], lsum[:, q], ALU.add).then_inc(mixb, 1)
                        n, q = i - 3, 1 - p
                        if live(n):
                            dve.wait_ge(lwhi_r, n + 1)
                            wait(dve, filled["Z1"], n - 1)
                            dve.tensor_tensor(lwT_lo[:, q], lwTf[:, q], lwT_hi[:, q], ALU.subtract).then_inc(lwlo_r, 1)
                        maxes(3)
                        n, q = i - 4, p
                        if live(n):
                            dve.wait_ge(mixhi_r, n + 1)
                            wait(dve, filled["WO"], n - 1)
                            dve.tensor_tensor(mix_lo[:, q], mix[:, q], mix_hi[:, q], ALU.subtract).then_inc(mixlo_r, 1)
                        n, q = i - 1, 1 - p
                        if live(n):
                            dve.wait_ge(filled["PJ2"], n + 1)
                            wait(dve, pv_ps, NG * (n - 1))
                            dve.tensor_tensor(vloc[:, q, :, 0:HD], bank_of["PJ2"][:, 0:D].rearrange("p (h d) -> p h d", h=NH),
                                              rows[:, 2 * D:3 * D].rearrange("p (h d) -> p h d", h=NH), ALU.add).then_inc(emptied["PJ2"], 1)
                            dve.wait_ge(filled["PJ3"], n + 1)
                            for k in range(KT):
                                dve.tensor_scalar(kq[:, q, D + k * P:D + (k + 1) * P], bank_of["PJ3"][:, k * P:(k + 1) * P],
                                                  vec[:, V_BQLIN + k:V_BQLIN + k + 1], None, ALU.add
                                                  ).then_inc(emptied["PJ3"] if k else kv_half, 1)
                        n, q = i - 1, 1 - p
                        if live(n):
                            dve.wait_ge(emptied["PJ4"], 2 * (n + 1))
                            wait(dve, sc_ps, NG * (n - 1))
                            dve.tensor_scalar(q_hi[:, q], qkf[:, q, 0], QK_SCALE, None, ALU.mult).then_inc(qhi_r, 1)
                            dve.wait_ge(qhi_r, n + 1)
                            dve.scalar_tensor_tensor(q_lo[:, q], qkf[:, q, 0], QK_SCALE, q_hi[:, q], ALU.mult, ALU.subtract).then_inc(qlo_r, 1)
                            dve.wait_ge(emptied["PJ5"], 2 * (n + 1))
                            for b in range(2):
                                dve.tensor_scalar(k_hi[:, q, :, b], qkf[:, q, 1], par[:, b:b + 1], None, ALU.mult).then_inc(khi_r, 1)
                            for b in range(2):
                                dve.wait_ge(khi_r, 2 * n + b + 1)
                                dve.scalar_tensor_tensor(k_lo[:, q, :, b], qkf[:, q, 1], par[:, b:b + 1], k_hi[:, q, :, b],
                                                         ALU.mult, ALU.subtract).then_inc(klo_r, 1)
                            dve.wait_ge(kq_ex, n + 1)
                            dve.scalar_tensor_tensor(kq[:, q], kq[:, q], 1.0, kq_exp[:, q], ALU.add, ALU.max).then_inc(kq_ready, 1)
                        n, q = i - 2, p
                        if live(n):
                            dve.wait_ge(filled["NUM"], n + 1)
                            wait(dve, emptied["NUM"], n - 1)
                            dve.tensor_scalar(den[:, q], bank_of["NUM"][:, D:D + 1], 1e-6, None, ALU.add).then_inc(den_r, 1)
                            dve.wait_ge(den_r, n + 1)
                            dve.reciprocal(rden[:, q], den[:, q]).then_inc(rden_r, 1)
                            dve.wait_ge(rden_r, n + 1)
                            wait(dve, filled["T2"], n - 1)
                            dve.tensor_scalar(lw[:, q, 0], bank_of["NUM"][:, 0:D], rden[:, q], None, ALU.mult).then_inc(emptied["NUM"], 1)
                        n, q = i - 3, 1 - p
                        if live(n):
                            dve.wait_ge(z1hi_r, n + 1)
                            wait(dve, filled["Z2"], n - 1)
                            dve.tensor_tensor(z1_lo[:, q], z1f[:, q], z1_hi[:, q], ALU.subtract).then_inc(z1lo_r, 1)
                        if isinstance(i, int):
                            for c in pieces_of_step(i):
                                low_part(c)

                    pipeline(dve, LAG, step)

                @block.tensor
                def _(pe):
                    pe.wait_ge(const_in, 64)
                    pe.wait_ge(w_lo_done, NPROJ)
                    pe.wait_ge(setup, 3)

                    def step(i, p, h):
                        if isinstance(i, int) and i == 3:
                            pe.wait_ge(w_lo_done, N1)
                        a, pa = i - 1, 1 - p
                        b, pb = i - 2, p
                        c, pc = i - 3, 1 - p
                        d, pd = i - 4, p

                        def hT(part, k):
                            t = hT_hi if part == 0 else hT_lo
                            return t[:, at(a), k].rearrange("p a t -> p (a t)")

                        def scores(g):
                            if live(b):
                                pe.wait_ge(qlo_r, b + 1)
                                pe.wait_ge(klo_r, 2 * (b + 1))
                                wait(pe, sc_rd, NG * b + g - 1)
                                s = slice(32 * g, 32 * g + 32)
                                for m in range(KT):
                                    o = sc_bank[g % 2][:, m * 2 * P:(m + 1) * 2 * P]
                                    for t, (qq, kk) in enumerate(((q_hi, k_hi), (q_hi, k_lo), (q_lo, k_hi))):
                                        last = pe.matmul(o, qq[s, pb, m], kk[s, pb, m].rearrange("p b t -> p (b t)"),
                                                         start=t == 0, stop=t == 2)
                                last.then_inc(sc_ps, 1)

                        def transposed(g):
                            n = b if g < NG // 2 else c
                            if live(n):
                                pe.wait_ge(sc_exp, NG * n + g + 1)
                                wait(pe, pT_rd, NG * n + g - 1)
                                for j in range(GH):
                                    last = pe.transpose(pT_bank[g % 2][:, j * P:(j + 1) * P], sc[:, g, j], ident[:])
                                last.then_inc(pT_ps, 1)

                        def weighted(g):
                            n, slot = (b, pb) if g < NG // 2 else (c, pc)
                            if live(n):
                                pe.wait_ge(pT_rd, NG * n + g + 1)
                                if g == 0:
                                    pe.wait_ge(emptied["PJ2"], b + 1)
                                    wait(pe, pv_rd, b)
                                for j, h in enumerate(group_heads(g)):
                                    last = pe.matmul(o_bank[:, h * (HD + 1):(h + 1) * (HD + 1)], pT[:, g % 2, j], vloc[:, slot, h],
                                                     start=True, stop=True)
                                last.then_inc(pv_ps, 1)

                        def token_major(u, col, width):
                            if live(a):
                                wait_turn(pe, u, i)
                                pe.wait_ge(hTlo_ready, a + 1)
                                t = 0
                                for hp, w in ((0, w_hi), (0, w_lo), (1, w_hi)):
                                    for k in range(KT):
                                        last = pe.matmul(bank_of[u][:, 0:width], hT(hp, k), w[:, k, col:col + width],
                                                         start=t == 0, stop=t == 5)
                                        t += 1
                                last.then_inc(filled[u], 1)

                        def feature_major(u, col):
                            if live(a):
                                wait_turn(pe, u, i)
                                pe.wait_ge(hTlo_ready, a + 1)
                                for m in range(KT):
                                    t = 0
                                    for w, hp in ((w_hi, 0), (w_lo, 0), (w_hi, 1)):
                                        for k in range(KT):
                                            last = pe.matmul(bank_of[u][:, m * P:(m + 1) * P],
                                                             w[:, k, col + m * P:col + (m + 1) * P], hT(hp, k),
                                                             start=t == 0, stop=t == 5)
                                            t += 1
                                last.then_inc(filled[u], 1)

                        scores(0)
                        transposed(2)
                        if live(a):
                            wait_turn(pe, "T", i)
                            pe.wait_ge(xn_ready, a + 1)
                            for k in range(KT):
                                last = pe.transpose(bank_of["T"][:, k * P:(k + 1) * P], xn[:, pa, k * P:(k + 1) * P], ident[:])
                            last.then_inc(filled["T"], 1)
                        scores(1)
                        weighted(2)
                        transposed(3)
                        if live(b):
                            pe.wait_ge(kq_ready, b + 1)
                            for k in range(KT):
                                wait_turn(pe, f"KV{k}", i)
                                pe.matmul(bank_of[f"KV{k}"][:, 0:D + 1], kq[:, pb, k * P:(k + 1) * P], vlin[:, pb], start=True, stop=True
                                          ).then_inc(filled[f"KV{k}"], 1)
                        if live(d):
                            wait_turn(pe, "Z2", i)
                            pe.wait_ge(z1lo_r, d + 1)
                            for m in range(KT):
                                t = 0
                                for w, z in ((w_hi, z1_hi), (w_lo, z1_hi), (w_hi, z1_lo)):
                                    for k in range(KT):
                                        last = pe.matmul(bank_of["Z2"][:, m * P:(m + 1) * P], w[:, k, C_WG2 + m * P:C_WG2 + (m + 1) * P],
                                                         z[:, pd, k], start=t == 0, stop=t == 5)
                                        t += 1
                            last.then_inc(filled["Z2"], 1)
                        weighted(3)
                        token_major("PJ1", C_KVLIN, 2 * D)
                        scores(2)
                        transposed(0)
                        token_major("PJ2", C_VLOC, D)
                        if live(c):
                            wait_turn(pe, "T2", i)
                            pe.wait_ge(emptied["NUM"], c + 1)
                            pe.wait_ge(pv_rd, c + 1)
                            for s in range(2):
                                for k in range(KT):
                                    last = pe.transpose(bank_of["T2"][:, (2 * s + k) * P:(2 * s + k + 1) * P],
                                                        lw[:, pc, s, k * P:(k + 1) * P], ident[:])
                            last.then_inc(filled["T2"], 1)
                        scores(3)
                        weighted(0)
                        transposed(1)
                        feature_major("PJ3", C_QLIN)
                        feature_major("PJ4", C_QLOC)
                        weighted(1)
                        feature_major("PJ5", C_KLOC)
                        if live(c):
                            wait_turn(pe, "Z1", i)
                            pe.wait_ge(lwlo_r, c + 1)
                            for m in range(KT):
                                t = 0
                                for w, hp in ((w_hi, 0), (w_lo, 0), (w_hi, 1)):
                                    for k in range(6):
                                        lo = hp == 1
                                        if k < 4:
                                            act_ = (lwT_lo if lo else lwT_hi)[:, pc, k]
                                        else:
                                            act_ = (hT_lo if lo else hT_hi)[:, at(c), k - 4].rearrange("p a t -> p (a t)")
                                        col = C_WG1 + (k // 2) * D + m * P
                                        last = pe.matmul(bank_of["Z1"][:, m * P:(m + 1) * P], w[:, k % 2, col:col + P], act_,
                                                         start=t == 0, stop=t == 17)
                                        t += 1
                            last.then_inc(filled["Z1"], 1)
                        if live(d):
                            wait_turn(pe, "WO", i)
                            pe.wait_ge(mixlo_r, d + 1)
                            t = 0
                            for m_, w in ((mix_hi, w_hi), (mix_hi, w_lo), (mix_lo, w_hi)):
                                for k in range(KT):
                                    last = pe.matmul(bank_of["WO"][:, 0:D], m_[:, pd, k], w[:, k, C_WO:C_WO + D], start=t == 0, stop=t == 5)
                                    t += 1
                            last.then_inc(filled["WO"], 1)
                        if live(b):
                            wait_turn(pe, "NUM", i)
                            pe.wait_ge(emptied["KV1"], b + 1)
                            for k in range(KT):
                                last = pe.matmul(bank_of["NUM"][:, 0:D + 1], kq[:, pb, D + k * P:D + (k + 1) * P], kvs[:, pb, k],
                                                 start=k == 0, stop=k == 1)
                            last.then_inc(filled["NUM"], 1)

                    pipeline(pe, LAG, step)


        of_stage1 = stage_sems[lasting:]
        c = Shared()
        c.sem, c.banks, c.x_rows, c.y_rows = sem, banks, x_rows, y_rows
        c.xs, c.xT_hi_all, c.xT_lo_all, c.w_hi, c.w_lo = xs, hT_hi, hT_lo, w2_hi, w2_lo
        c.ident, c.par, c.neghalf = ident, par, neghalf
        c.tri, c.rbias = sb("tri", [P, P]), sb("rbias", [P, NE])
        c.ones = sb("ones", [P, P])
        c.we_hi, c.we_lo = sb("we_hi", [P, NE, EW], F16), sb("we_lo", [P, NE, EW], F16)
        c.wt, c.pos, c.sel = sb("wt", [P, NB, NE]), sb("pos", [P, NB, NE]), sb("sel", [P, NB, NE])
        c.count = sb("count", [P, NE])
        c.zeroed = zeroed
        c.we_lo_done = sem("we_lo_done")
        c.dve_passed, c.pool_passed = dve_passed, pool_passed
        cross_attention(nc, c, ctx_t, experts, consts, rbias_d, out)
        nc.all_engine_barrier()
        nc.clear_and_free_semaphores(of_stage1)
        nc.all_engine_barrier()
        expert_layer(nc, c, consts, out)


class Shared:
    pass


def chain(eng, sem, per, n):
    done = [0]

    def link(instruction):
        done[0] += 1
        instruction.then_inc(sem, 1)
        eng.wait_ge(sem, per * n + done[0])
        assert done[0] <= per
    return link


def half(h, p, lag):
    return h + (p - lag) // 2


def cross_attention(nc, c, ctx_t, experts, consts, rbias_d, out):
    sem, banks, xs, w_hi, w_lo, ident, par, neghalf = c.sem, c.banks, c.xs, c.w_hi, c.w_lo, c.ident, c.par, c.neghalf
    ctx_tiles = ctx_t.rearrange("(k p) (b t) -> p k b t", p=P, t=P)
    shared = c

    with ExitStack() as st:
        def s2(name, shape, dt=F32):
            return st.enter_context(nc.sbuf_tensor(name, shape, dt))

        cst = s2("cst", [P, 2, KT, P])
        c_hi = s2("c_hi", [P, 2, KT, P], F16)
        c_lo = s2("c_lo", [P, 2, KT, P], F16)
        xcur = s2("xcur", [P, 2, D])
        xT_hi = s2("xT_hi", [P, 2, KT, P], F16)
        xT_lo = s2("xT_lo", [P, 2, KT, P], F16)
        xq_hi = s2("xq_hi", [P, 2, KT, P], F16)
        xq_lo = s2("xq_lo", [P, 2, KT, P], F16)
        xk_hi = s2("xk_hi", [P, 2, KT, 2, P], F16)
        xk_lo = s2("xk_lo", [P, 2, KT, 2, P], F16)
        xv = s2("xv", [P, 2, NH, HD + 1])
        scx = s2("scx", [P, NG, GH, P])
        mxx = s2("mxx", [P, NG, GH])
        pTx = s2("pTx", [P, 2, GH, P])
        rsx = s2("rsx", [P, 2, NH])
        ao = s2("ao", [P, 2, D])
        aT_hi = s2("aT_hi", [P, 2, KT, P], F16)
        aT_lo = s2("aT_lo", [P, 2, KT, P], F16)
        yx = s2("yx", [P, 2, D])
        xstats = s2("xstats", [P, 2, 6])
        xmv = s2("xmv", [P, 2, 2])
        xvar = s2("xvar", [P, 2, 1])
        xrstd = s2("xrstd", [P, 2, 1])

        sc_bank, pT_bank, o_bank, turn = banks[0:2], banks[2:4], banks[4], banks[5:8]
        ORDER = ["CN", "LG", "XWO", "XPK", "XPQ", "XPV", "XT", "XT2", "T3"]
        LAGS = {"XT": 0, "XT2": 3, "XWO": 4, "XPK": 1, "XPQ": 1, "XPV": 1, "LG": 6, "T3": 5, "CN": 7}
        bank_of = {u: turn[k % 3] for k, u in enumerate(ORDER)}
        filled = {u: sem(f"ps_{u}") for u in ORDER}
        emptied = {u: sem(f"rd_{u}") for u in ORDER}
        wait_turn = Turns(ORDER, LAGS, {"XPK": 2}, emptied).wait

        east = s2("east", [P, 2, EW])
        x2c = s2("x2c", [P, 2, D])
        rt_e = s2("rt_e", [P, 2, NE])
        rt_e1 = s2("rt_e1", [P, 2, NE])
        score = s2("score", [P, 2, NE])
        sfc = s2("sfc", [P, 2, NE])
        g8 = s2("g8", [P, 2, NGRP, 8])
        gsum = s2("gsum", [P, 2, NGRP + 8])
        gtop = s2("gtop", [P, 2, 8])
        grep = s2("grep", [P, 2, 8])
        gout = s2("gout", [P, 2, NGRP + 8])
        gmask = s2("gmask", [P, 2, NGRP])
        cand = s2("cand", [P, 2, NE + 8])
        ctop = s2("ctop", [P, 2, 8])
        crep = s2("crep", [P, 2, 8])
        cout = s2("cout", [P, 2, NE + 8])
        wraw = s2("wraw", [P, 2, NE])
        wsum = s2("wsum", [P, 2, 1])
        winv = s2("winv", [P, 2, 1])
        selc = s2("selc", [P, 2, NE])

        ones_set = sem("x_ones_set")
        ctx_in = [sem(f"ctx_in{k}") for k in range(2)]
        we_in = [sem(f"we_in{k}") for k in range(2)]
        rc_in = sem("rc_in")
        we_hi_done = sem("we_hi_done")
        x2c_ready, x2Thi_r = sem("x2c_ready"), sem("x2Thi_r")
        sel_r = sem("sel_r")
        route_step, pos_r = sem("route_step"), sem("pos_r")
        g8_part = sem("g8_part")
        ROUTE_STEPS, SEL_LINK = 18, 14
        chi_r, clo_r = sem("chi_r"), sem("clo_r")
        xThi_r, xcur_r = sem("xThi_r"), sem("xcur_r")
        xqhi_r = sem("xqhi_r")
        xkhi_r = sem("xkhi_r")
        xsc_ps, xmx_r, xsc_rd, xsc_exp = sem("xsc_ps"), sem("xmx_r"), sem("xsc_rd"), sem("xsc_exp")
        xpT_ps, xpT_rd = sem("xpT_ps"), sem("xpT_rd")
        xpv_ps, xpv_rec, xpv_rd = sem("xpv_ps"), sem("xpv_rec"), sem("xpv_rd")
        aThi_r = sem("aThi_r")
        xln_stat, xln_mv, xln_var, xln_rstd = sem("xln_stat"), sem("xln_mv"), sem("xln_var"), sem("xln_rstd")
        x2_ready = sem("x2_ready")
        LAG = 8

        with nc.Block() as block:
            @block.sync
            def _(sp):
                sp.dma_start(shared.tri[:], consts[:, P:2 * P]).then_inc(rc_in, 16)
                sp.dma_start(shared.rbias[:], rbias_d.rearrange("(a n) -> a n", a=1).broadcast_to([P, NE])).then_inc(rc_in, 16)

                def step(i, p, h):
                    wait(sp, clo_r, i - 1)
                    sp.dma_start(cst[:, p], ctx_tiles[:, :, at(i)].rearrange("p k a t -> p k (a t)")).then_inc(ctx_in[p], 16)
                    for q in range(2):
                        wait(sp, shared.we_lo_done, i * 2 + q - 1)
                        sp.dma_start(east[:, q], experts[:, at(i * 2 + q)].rearrange("p a w -> p (a w)")).then_inc(we_in[q], 16)

                pipeline(sp, 0, step)

            @block.gpsimd
            def _(pool):
                for t, v in ((xv[:, :, :, HD:HD + 1], 1.0), (shared.ones[:], 1.0), (gsum[:, :, NGRP:], PAD),
                             (grep[:], PAD), (cand[:, :, NE:], PAD), (crep[:], PAD), (shared.count[:], 0.0)):
                    pool.memset(t, v).then_inc(ones_set, 1)

                def step(i, p, h):
                    n = i
                    if live(n):
                        wait(pool, filled["XT"], n - 1)
                        pool.tensor_copy(xcur[:, p], xs[:, at(n)].rearrange("p a d -> p (a d)")).then_inc(xcur_r, 1)
                    n, q = i - 4, p
                    if live(n):
                        wait(pool, xln_var, n + 1)
                        wait(pool, x2c_ready, n - 1)
                        pool.tensor_tensor(xrstd[:, q], xvar[:, q], neghalf[:], ALU.pow).then_inc(xln_rstd, 1)
                        pool.wait_ge(x2c_ready, n + 1)
                        pool.tensor_copy(xs[:, at(n)].rearrange("p a d -> p (a d)"), x2c[:, q]).then_inc(x2_ready, 1)
                    n = i
                    if live(n):
                        for k in range(2):
                            pool.wait_ge(we_hi_done, 2 * n + k + 1)
                            pool.tensor_tensor(shared.we_lo[:, at(n * 2 + k)].rearrange("p a w -> p (a w)"), east[:, k],
                                               shared.we_hi[:, at(n * 2 + k)].rearrange("p a w -> p (a w)"), ALU.subtract
                                               ).then_inc(shared.we_lo_done, 1)

                pipeline(pool, LAG, step)

            @block.scalar
            def _(act):
                def step(i, p, h):
                    def exps(g):
                        n = i - 2
                        if live(n):
                            act.wait_ge(xsc_rd, NG * n + g + 1)
                            act.activation(scx[:, g], scx[:, g], ACT.Exp).then_inc(xsc_exp, 1)

                    def probabilities(g):
                        n = i - 2 if g < NG // 2 else i - 3
                        if live(n):
                            act.wait_ge(xpT_ps, NG * n + g + 1)
                            wait(act, xpv_ps, NG * n + g - 1)
                            act.activation(pTx[:, g % 2], pT_bank[g % 2][:].rearrange("p (h k) -> p h k", h=GH), ACT.Copy
                                           ).then_inc(xpT_rd, 1)

                    probabilities(2)
                    probabilities(3)
                    exps(0)
                    exps(1)
                    n, q = i - 6, p
                    if live(n):
                        act.wait_ge(filled["LG"], n + 1)
                        wait(act, route_step, ROUTE_STEPS * (n - 2) + 1)
                        act.activation(rt_e[:, q], bank_of["LG"][:, 0:NE], ACT.Exp, scale=-1.0).then_inc(emptied["LG"], 1)
                    n = i
                    if live(n):
                        wait(act, filled["XPV"], n - 1)
                        act.wait_ge(ctx_in[p], 16 * (h + 1))
                        act.activation(c_hi[:, p], cst[:, p], ACT.Copy).then_inc(chi_r, 1)
                        act.wait_ge(we_in[0], 16 * (n + 1))
                        act.activation(shared.we_hi[:, at(n * 2)].rearrange("p a w -> p (a w)"), east[:, 0], ACT.Copy).then_inc(we_hi_done, 1)
                    n, q = i - 1, 1 - p
                    if live(n):
                        act.wait_ge(filled["XPK"], n + 1)
                        wait(act, xsc_ps, NG * (n - 1))
                        for b in range(2):
                            act.activation(xk_hi[:, q, :, b], bank_of["XPK"][:, 0:D].rearrange("p (k t) -> p k t", k=KT), ACT.Copy,
                                           scale=par[:, b:b + 1]).then_inc(xkhi_r, 1)
                    exps(2)
                    probabilities(0)
                    if live(n):
                        act.wait_ge(filled["XPQ"], n + 1)
                        act.activation(xq_hi[:, q], bank_of["XPQ"][:, 0:D].rearrange("p (k t) -> p k t", k=KT), ACT.Copy,
                                       scale=QK_SCALE).then_inc(xqhi_r, 1)
                    exps(3)
                    probabilities(1)
                    if live(n):
                        act.wait_ge(filled["XPV"], n + 1)
                        wait(act, xpv_ps, NG * (n - 1))
                        act.activation(xv[:, q, :, 0:HD], bank_of["XPV"][:, 0:D].rearrange("p (h d) -> p h d", h=NH), ACT.Copy
                                       ).then_inc(emptied["XPV"], 1)
                    n = i
                    if live(n):
                        act.wait_ge(filled["XT"], n + 1)
                        wait(act, filled["XPQ"], n - 1)
                        act.activation(xT_hi[:, p], bank_of["XT"][:, 0:D].rearrange("p (k t) -> p k t", k=KT), ACT.Copy).then_inc(xThi_r, 1)
                    n, q = i - 3, 1 - p
                    if live(n):
                        act.wait_ge(filled["XT2"], n + 1)
                        wait(act, filled["XWO"], n - 1)
                        act.activation(aT_hi[:, q], bank_of["XT2"][:, 0:D].rearrange("p (k t) -> p k t", k=KT), ACT.Copy).then_inc(aThi_r, 1)
                    n = i - 5
                    if live(n):
                        act.wait_ge(filled["T3"], n + 1)
                        act.activation(shared.xT_hi_all[:, at(n)].rearrange("p a k t -> p (a k t)"), bank_of["T3"][:, 0:D], ACT.Copy
                                       ).then_inc(x2Thi_r, 1)
                    n = i
                    if live(n):
                        act.wait_ge(we_in[1], 16 * (n + 1))
                        act.activation(shared.we_hi[:, at(n * 2 + 1)].rearrange("p a w -> p (a w)"), east[:, 1], ACT.Copy).then_inc(we_hi_done, 1)

                pipeline(act, LAG, step)

            @block.vector
            def _(dve):
                dve.wait_ge(rc_in, 32)
                dve.wait_ge(ones_set, 7)

                def step(i, p, h):
                    def soft(g):
                        n = i - 2
                        if live(n):
                            ps = sc_bank[g % 2][:].rearrange("p (h k) -> p h k", h=GH)
                            dve.wait_ge(xsc_ps, NG * n + g + 1)
                            wait(dve, xsc_rd, NG * (n - 1) + g + 1)
                            dve.reduce_max(mxx[:, g], ps, AX_X).then_inc(xmx_r, 1)
                            dve.wait_ge(xmx_r, NG * n + g + 1)
                            wait(dve, xpT_ps, NG * (n - 1) + g + 1)
                            dve.tensor_tensor(scx[:, g], ps, mxx[:, g].unsqueeze(2).to_broadcast([P, GH, P]), ALU.subtract
                                              ).then_inc(xsc_rd, 1)

                    soft(0)
                    n, q = i - 7, 1 - p
                    if live(n):
                        one = at(n)
                        flat = "p a e -> p (a e)"
                        dve.wait_ge(filled["CN"], n + 1)
                        dve.tensor_tensor(shared.pos[:, one].rearrange(flat), bank_of["CN"][:, 0:NE], shared.count[:], ALU.add).then_inc(pos_r, 1)
                        dve.wait_ge(pos_r, n + 1)
                        dve.tensor_tensor(shared.count[:], bank_of["CN"][:, NE:2 * NE], shared.count[:], ALU.add).then_inc(emptied["CN"], 1)
                        dve.wait_ge(emptied["CN"], n + 1)
                    soft(1)
                    n, q = i - 4, p
                    if live(n):
                        xt = xs[:, at(n)].rearrange("p a d -> p (a d)")
                        dve.wait_ge(filled["XWO"], n + 1)
                        wait(dve, x2c_ready, n - 1)
                        dve.tensor_tensor(yx[:, q], bank_of["XWO"][:, 0:D], xt, ALU.add).then_inc(emptied["XWO"], 1)
                        dve.wait_ge(emptied["XWO"], n + 1)
                        wait(dve, xln_mv, n - 1)
                        dve.bn_stats(xstats[:, q], yx[:, q]).then_inc(xln_stat, 1)
                        dve.wait_ge(xln_stat, n + 1)
                        wait(dve, x2c_ready, n - 1)
                        settle(dve, n, shared.dve_passed, rc_in, 32)
                        dve.bn_aggr(xmv[:, q], xstats[:, q]).then_inc(xln_mv, 1)
                        dve.wait_ge(xln_mv, n + 1)
                        wait(dve, xln_rstd, n - 1)
                        dve.tensor_scalar(xvar[:, q], xmv[:, q, 1:2], LN_EPS, None, ALU.add).then_inc(xln_var, 1)
                    n, q = i - 3, 1 - p
                    if live(n):
                        o = o_bank[:, 0:NH * (HD + 1)].rearrange("p (h d) -> p h d", h=NH)
                        dve.wait_ge(xpv_ps, NG * (n + 1))
                        wait(dve, xpv_rd, n - 1)
                        dve.reciprocal(rsx[:, q], o[:, :, HD]).then_inc(xpv_rec, 1)
                        dve.wait_ge(xpv_rec, n + 1)
                        wait(dve, filled["XT2"], n - 1)
                        dve.tensor_tensor(ao[:, q].rearrange("p (h d) -> p h d", h=NH), o[:, :, 0:HD],
                                          rsx[:, q].unsqueeze(2).to_broadcast([P, NH, HD]), ALU.mult).then_inc(xpv_rd, 1)
                    n = i
                    if live(n):
                        dve.wait_ge(chi_r, n + 1)
                        wait(dve, filled["XPV"], n - 1)
                        dve.tensor_tensor(c_lo[:, p], cst[:, p], c_hi[:, p], ALU.subtract).then_inc(clo_r, 1)
                    soft(2)
                    n, q = i - 4, p
                    if live(n):
                        dve.wait_ge(xln_rstd, n + 1)
                        wait(dve, filled["T3"], n - 1)
                        wait(dve, x2_ready, n - 1)
                        dve.tensor_scalar(x2c[:, q], yx[:, q], xmv[:, q, 0:1], xrstd[:, q],
                                          ALU.subtract, ALU.mult).then_inc(x2c_ready, 1)
                        dve.wait_ge(x2c_ready, n + 1)
                    n, q = i - 1, 1 - p
                    if live(n):
                        wait(dve, xsc_ps, NG * (n - 1))
                        for b in range(2):
                            dve.wait_ge(xkhi_r, 2 * (n + 1))
                            dve.scalar_tensor_tensor(xk_lo[:, q, :, b], bank_of["XPK"][:, 0:D].rearrange("p (k t) -> p k t", k=KT),
                                                     par[:, b:b + 1], xk_hi[:, q, :, b], ALU.mult, ALU.subtract).then_inc(emptied["XPK"], 1)
                    soft(3)
                    n, q = i - 1, 1 - p
                    if live(n):
                        dve.wait_ge(xqhi_r, n + 1)
                        dve.scalar_tensor_tensor(xq_lo[:, q], bank_of["XPQ"][:, 0:D].rearrange("p (k t) -> p k t", k=KT), QK_SCALE,
                                                 xq_hi[:, q], ALU.mult, ALU.subtract).then_inc(emptied["XPQ"], 1)
                    n, q = i - 6, p
                    if live(n):
                        link = chain(dve, route_step, ROUTE_STEPS, n)
                        dve.wait_ge(emptied["LG"], n + 1)
                        link(dve.tensor_scalar(rt_e1[:, q], rt_e[:, q], 1.0, None, ALU.add))
                        link(dve.reciprocal(score[:, q], rt_e1[:, q]))
                        link(dve.tensor_tensor(sfc[:, q], score[:, q], shared.rbias[:], ALU.add))
                        for g in range(NGRP):
                            settle(dve, n if g == 0 else 0, shared.dve_passed, rc_in, 32)
                            last = dve.max(g8[:, q, g], sfc[:, q, g * EG:(g + 1) * EG])
                            if g < NGRP - 1:
                                last.then_inc(g8_part, 1)
                        link(last)
                        dve.wait_ge(g8_part, (NGRP - 1) * (n + 1))
                        link(dve.tensor_tensor(gsum[:, q, 0:NGRP], g8[:, q, :, 0], g8[:, q, :, 1], ALU.add))
                        settle(dve, n, shared.dve_passed, rc_in, 32)
                        link(dve.max(gtop[:, q], gsum[:, q]))
                        link(dve.tensor_copy(grep[:, q, 0:2], gtop[:, q, 0:2]))
                        settle(dve, n, shared.dve_passed, rc_in, 32)
                        link(dve.match_replace(gout[:, q], grep[:, q], gsum[:, q], TAKEN))
                        link(dve.tensor_scalar(gmask[:, q], gout[:, q, 0:NGRP], TAKEN, None, ALU.is_equal))
                        link(dve.tensor_tensor(cand[:, q, 0:NE].rearrange("p (g e) -> p g e", g=NGRP),
                                               sfc[:, q].rearrange("p (g e) -> p g e", g=NGRP),
                                               gmask[:, q].unsqueeze(2).to_broadcast([P, NGRP, EG]), ALU.mult))
                        settle(dve, n, shared.dve_passed, rc_in, 32)
                        link(dve.max(ctop[:, q], cand[:, q]))
                        link(dve.tensor_copy(crep[:, q, 0:TOPK], ctop[:, q, 0:TOPK]))
                        settle(dve, n, shared.dve_passed, rc_in, 32)
                        link(dve.match_replace(cout[:, q], crep[:, q], cand[:, q], TAKEN))
                        wait(dve, filled["CN"], n - 1)
                        link(dve.tensor_scalar(selc[:, q], cout[:, q, 0:NE], TAKEN, None, ALU.is_equal))
                        dve.tensor_copy(shared.sel[:, at(n)].rearrange("p a e -> p (a e)"), selc[:, q]).then_inc(sel_r, 1)
                        link(dve.scalar_tensor_tensor(wraw[:, q], cout[:, q, 0:NE], TAKEN, score[:, q], ALU.is_equal, ALU.mult,
                                                      accum_out=wsum[:, q]))
                        link(dve.tensor_scalar(wsum[:, q], wsum[:, q], 1e-20, None, ALU.add))
                        link(dve.reciprocal(winv[:, q], wsum[:, q]))
                        link(dve.tensor_scalar(shared.wt[:, at(n)].rearrange("p a e -> p (a e)"), wraw[:, q], winv[:, q], ROUTE_SCALE,
                                               ALU.mult, ALU.mult))
                        dve.wait_ge(sel_r, n + 1)
                    n = i
                    if live(n):
                        dve.wait_ge(xThi_r, n + 1)
                        wait(dve, filled["XPQ"], n - 1)
                        dve.tensor_tensor(xT_lo[:, p], bank_of["XT"][:, 0:D].rearrange("p (k t) -> p k t", k=KT), xT_hi[:, p], ALU.subtract
                                          ).then_inc(emptied["XT"], 1)
                    n, q = i - 3, 1 - p
                    if live(n):
                        dve.wait_ge(aThi_r, n + 1)
                        wait(dve, filled["XWO"], n - 1)
                        dve.tensor_tensor(aT_lo[:, q], bank_of["XT2"][:, 0:D].rearrange("p (k t) -> p k t", k=KT), aT_hi[:, q], ALU.subtract
                                          ).then_inc(emptied["XT2"], 1)
                    n = i - 5
                    if live(n):
                        dve.wait_ge(x2Thi_r, n + 1)
                        one = at(n)
                        dve.tensor_tensor(shared.xT_lo_all[:, one].rearrange("p a k t -> p (a k t)"), bank_of["T3"][:, 0:D],
                                          shared.xT_hi_all[:, one].rearrange("p a k t -> p (a k t)"), ALU.subtract).then_inc(emptied["T3"], 1)

                pipeline(dve, LAG, step)

            @block.tensor
            def _(pe):
                pe.wait_ge(ones_set, 7)
                pe.wait_ge(rc_in, 32)

                def step(i, p, h):
                    n, a, b, c, d = i, i - 1, i - 2, i - 3, i - 4
                    pa, pb, pc, pd = 1 - p, p, 1 - p, p

                    def scores(g):
                        if live(b):
                            pe.wait_ge(emptied["XPQ"], b + 1)
                            pe.wait_ge(emptied["XPK"], 2 * (b + 1))
                            wait(pe, xsc_rd, NG * b + g - 1)
                            s = slice(32 * g, 32 * g + 32)
                            for m in range(KT):
                                o = sc_bank[g % 2][:, m * 2 * P:(m + 1) * 2 * P]
                                for t, (qq, kk) in enumerate(((xq_hi, xk_hi), (xq_hi, xk_lo), (xq_lo, xk_hi))):
                                    last = pe.matmul(o, qq[s, pb, m], kk[s, pb, m].rearrange("p b t -> p (b t)"),
                                                     start=t == 0, stop=t == 2)
                            last.then_inc(xsc_ps, 1)

                    def transposed(g):
                        t, slot = (b, pb) if g < NG // 2 else (c, pc)
                        if live(t):
                            pe.wait_ge(xsc_exp, NG * t + g + 1)
                            wait(pe, xpT_rd, NG * t + g - 1)
                            for j in range(GH):
                                last = pe.transpose(pT_bank[g % 2][:, j * P:(j + 1) * P], scx[:, g, j], ident[:])
                            last.then_inc(xpT_ps, 1)

                    def weighted(g):
                        t, slot = (b, pb) if g < NG // 2 else (c, pc)
                        if live(t):
                            pe.wait_ge(xpT_rd, NG * t + g + 1)
                            if g == 0:
                                pe.wait_ge(emptied["XPV"], t + 1)
                                wait(pe, xpv_rd, t)
                            for j, h in enumerate(group_heads(g)):
                                last = pe.matmul(o_bank[:, h * (HD + 1):(h + 1) * (HD + 1)], pTx[:, g % 2, j], xv[:, slot, h],
                                                 start=True, stop=True)
                            last.then_inc(xpv_ps, 1)

                    def products(u, lhs, rhs, tiles, width):
                        for m in range(tiles):
                            t = 0
                            for x_, y_ in ((0, 0), (0, 1), (1, 0)):
                                for k in range(KT):
                                    last = pe.matmul(bank_of[u][:, m * width:(m + 1) * width], lhs(x_, k, m), rhs(y_, k, m),
                                                     start=t == 0, stop=t == 5)
                                    t += 1
                        last.then_inc(filled[u], 1)

                    W = (w_hi, w_lo)
                    C = (c_hi, c_lo)
                    X = (xT_hi, xT_lo)
                    Z = (shared.xT_hi_all, shared.xT_lo_all)
                    e, f = i - 5, i - 6
                    scores(0)
                    transposed(2)
                    g7 = i - 7
                    if live(g7):
                        wait_turn(pe, "CN", i)
                        pe.wait_ge(route_step, ROUTE_STEPS * g7 + SEL_LINK)
                        pe.matmul(bank_of["CN"][:, 0:NE], shared.tri[:], selc[:, 1 - p], start=True, stop=True)
                        pe.matmul(bank_of["CN"][:, NE:2 * NE], shared.ones[:], selc[:, 1 - p], start=True, stop=True
                                  ).then_inc(filled["CN"], 1)
                    scores(1)
                    weighted(2)
                    transposed(3)
                    if live(f):
                        wait_turn(pe, "LG", i)
                        pe.wait_ge(emptied["T3"], f + 1)
                        products("LG", lambda s, k, m: Z[s][:, at(f), k].rearrange("p a t -> p (a t)"),
                                 lambda s, k, m: W[s][:, k, C_RT:C_RT + NE], 1, NE)
                    if live(d):
                        wait_turn(pe, "XWO", i)
                        pe.wait_ge(emptied["XT2"], d + 1)
                        A = (aT_hi, aT_lo)
                        products("XWO", lambda s, k, m: A[s][:, pd, k], lambda s, k, m: W[s][:, k, C_XO:C_XO + D], 1, D)
                    weighted(3)
                    if live(a):
                        wait_turn(pe, "XPK", i)
                        pe.wait_ge(clo_r, a + 1)
                        products("XPK", lambda s, k, m: W[s][:, k, C_XK + m * P:C_XK + (m + 1) * P], lambda s, k, m: C[s][:, pa, k], KT, P)
                    scores(2)
                    transposed(0)
                    if live(a):
                        wait_turn(pe, "XPQ", i)
                        pe.wait_ge(emptied["XT"], a + 1)
                        products("XPQ", lambda s, k, m: W[s][:, k, C_XQ + m * P:C_XQ + (m + 1) * P], lambda s, k, m: X[s][:, pa, k], KT, P)
                    scores(3)
                    weighted(0)
                    transposed(1)
                    if live(a):
                        wait_turn(pe, "XPV", i)
                        products("XPV", lambda s, k, m: C[s][:, pa, k], lambda s, k, m: W[s][:, k, C_XV:C_XV + D], 1, D)
                    weighted(1)
                    if live(n):
                        wait_turn(pe, "XT", i)
                        pe.wait_ge(xcur_r, n + 1)
                        for k in range(KT):
                            last = pe.transpose(bank_of["XT"][:, k * P:(k + 1) * P], xcur[:, p, k * P:(k + 1) * P], ident[:])
                        last.then_inc(filled["XT"], 1)
                    if live(c):
                        wait_turn(pe, "XT2", i)
                        pe.wait_ge(xpv_rd, c + 1)
                        for k in range(KT):
                            last = pe.transpose(bank_of["XT2"][:, k * P:(k + 1) * P], ao[:, pc, k * P:(k + 1) * P], ident[:])
                        last.then_inc(filled["XT2"], 1)
                    if live(e):
                        wait_turn(pe, "T3", i)
                        pe.wait_ge(x2c_ready, e + 1)
                        for k in range(KT):
                            last = pe.transpose(bank_of["T3"][:, k * P:(k + 1) * P], x2c[:, 1 - p, k * P:(k + 1) * P], ident[:])
                        last.then_inc(filled["T3"], 1)

                pipeline(pe, LAG, step)


def expert_layer(nc, c, consts, out):
    sem, banks, xs, W, ident, neghalf = c.sem, c.banks, c.xs, (c.w_hi, c.w_lo), c.ident, c.neghalf
    X = (c.xT_hi_all, c.xT_lo_all)
    E = (c.we_hi, c.we_lo)
    CT = 2
    NCH = NB // CT
    CW = CT * P
    U = 4
    LAG3 = 6
    SP_LAG = 10
    EDGE = 8
    SPLIT = 4
    YS = 2

    with ExitStack() as st:
        def s3(name, shape, dt=F32):
            return st.enter_context(nc.sbuf_tensor(name, shape, dt))

        known = s3("known", [P, 1 + NE])
        place, eid = known[:, 0:1], known[:, 1:]
        thr = s3("thr", [P, NB])
        over = s3("over", [P, NE, NB])
        PADC = NE // 2
        cums = s3("cums", [P, 2, PADC + NE])
        base = s3("base", [P, NE])
        after = s3("after", [P, NE])
        diag = s3("diag", [P, P])
        owner = s3("owner", [P, 1])
        tile_e = s3("tile_e", [P, EDGE + NT + EDGE], U32)
        sgate = s3("sgate", [P, 2, KT, CW])
        shid = s3("shid", [P, 2, KT, CW])
        sh_hi = s3("sh_hi", [P, 2, KT, CW], F16)
        sh_lo = s3("sh_lo", [P, 2, KT, CW], F16)
        ident16 = s3("ident16", [P, P], F16)
        xg = s3("xg", [P, U, 2, KT, P], F16)
        gT = s3("gT", [P, U, 2, KT, P], F16)
        eg = s3("eg", [P, U, EI])
        eh = s3("eh", [P, U, EI])
        eh_hi = s3("eh_hi", [P, U, EI], F16)
        eh_lo = s3("eh_lo", [P, U, EI], F16)
        yo = s3("yo", [P, U, D])
        ykey = s3("ykey", [P, NB, NE])
        y8 = s3("y8", [P, NB, 8])
        same = s3("same", [P, NB, NE])
        y_ix = s3("y_ix", [P, NB, TOPK], U32)
        y_w = s3("y_w", [P, NB, TOPK])
        y_wc = s3("y_wc", [P, 2, TOPK])
        fstats = s3("fstats", [P, 2, 6])
        fmv = s3("fmv", [P, 2, 2])
        fvar = s3("fvar", [P, 2, 1])
        frstd = s3("frstd", [P, 2, 1])

        with ExitStack() as before_tiles:
            xhl = before_tiles.enter_context(nc.sbuf_tensor("xhl", [P, NB, 2, D], F16))
        yg = s3("yg", [P, YS, TOPK, D])
        ysum = s3("ysum", [P, 2, D])
        fin = s3("fin", [P, 2, D])

        k_in = sem("k_in")
        xhi_r, xlo_r, id16_r = sem("xhi_r"), sem("xlo_r"), sem("id16_r")
        pads = sem("pads")
        y_ix_ready, scattered, weight_step = sem("y_ix_ready"), sem("scattered"), sem("weight_step")
        tab_step, tab_ps, tab_ready = sem("tab_step"), sem("tab_ps"), sem("tab_ready")
        sg_ps, su_ps, sd_ps = sem("sg_ps"), sem("su_ps"), sem("sd_ps")
        sg_r, shid_r, shhi_r, shlo_r, sacc_r = sem("sg_r"), sem("shid_r"), sem("shhi_r"), sem("shlo_r"), sem("sacc_r")
        gathered = [sem(f"gathered{k}") for k in range(U)]
        gt_ps, gt_r = sem("gt_ps"), sem("gt_r")
        gu_ps, eg_r, eh_r, ehhi_r, ehlo_r = sem("gu_ps"), sem("eg_r"), sem("eh_r"), sem("ehhi_r"), sem("ehlo_r")
        dn_ps, yo_r = sem("dn_ps"), sem("yo_r")
        stored = [sem(f"stored{k}") for k in range(U)]
        y8_part = sem("y8_part")
        ywc_r = sem("ywc_r")
        ygathered = [sem(f"ygathered{k}") for k in range(YS)]
        ysum_step, f_stat, f_mv, f_var, f_rstd, fin_r = (sem("ysum_step"), sem("f_stat"), sem("f_mv"), sem("f_var"),
                                                         sem("f_rstd"), sem("fin_r"))
        sent = [sem(f"sent{k}") for k in range(2)]

        G_BANK, U_BANK, D_BANK = banks[0:2], banks[2:4], banks[4:6]
        TAB_BANK = banks[6]
        GT_BANK = [b[:].bitcast(F16)[:, 0:2 * D].rearrange("p (s k t) -> p s k t", s=2, k=KT) for b in banks[6:8]]
        GU_BANK, DN_BANK = banks[0:4], banks[4:6]

        with nc.Block() as block:
            @block.sync
            def _(sp):
                sp.dma_start(known[:], consts[:, 2 * P + NE:2 * P + 2 * NE + 1]).then_inc(k_in, 16)

                sp.wait_ge(scattered, 16 * NB * TOPK)

                def tile(i, s, h):
                    n = i
                    if live(n, NT):
                        wait(sp, gt_ps, n - U + 1)
                        sp.dma_start(xg[:, s].rearrange("p s k t -> p (s k t)"), c.x_rows[bass.ds(n * P, P), :]).then_inc(gathered[s], 16)
                    n, q = i - SP_LAG, (s - SP_LAG) % U
                    if live(n, NT):
                        sp.wait_ge(yo_r, n + 1)
                        sp.dma_start(c.y_rows[bass.ds(n * P, P), :], yo[:, q]).then_inc(stored[q], 16)

                pipeline(sp, SP_LAG, tile, NT, U)

                def final(i, p, h):
                    sp.wait_ge(fin_r, i + 1)
                    sp.dma_start(out[at(i)].rearrange("a p d -> p (a d)"), fin[:, p]).then_inc(sent[p], 16)

                pipeline(sp, 0, final)
                for p in range(2):
                    sp.wait_ge(sent[p], 16 * NB // 2)

            @block.gpsimd
            def _(pool):
                pool.memset(cums[:, :, 0:PADC], 0.0).then_inc(pads, 1)
                pool.memset(tile_e[:], 0).then_inc(pads, 1)
                pool.wait_ge(c.zeroed, 16 * NZ)
                pool.wait_ge(y_ix_ready, 1)
                for n in range(NB):
                    pool.wait_ge(xlo_r, n // SPLIT + 1)
                    for k in range(TOPK):
                        pool.indirect_dma_start(c.x_rows, bass.IndirectOffsetOnAxis(ap=y_ix[:, n, k:k + 1], axis=0),
                                                xhl[:, n].rearrange("p s d -> p (s d)"), None).then_inc(scattered, 16)
                for s in range(U):
                    pool.wait_ge(stored[s], 16 * NT // U)
                for n in range(NB + 1):
                    if n < NB:
                        wait(pool, ysum_step, SUM_STEPS * (n - YS + 1))
                        for k in range(TOPK):
                            pool.indirect_dma_start(yg[:, n % YS, k], None, c.y_rows,
                                                    bass.IndirectOffsetOnAxis(ap=y_ix[:, n, k:k + 1], axis=0)
                                                    ).then_inc(ygathered[n % YS], 16)
                    if n > 0:
                        m = n - 1
                        pool.wait_ge(f_var, m + 1)
                        wait(pool, fin_r, m - 1)
                        pool.tensor_tensor(frstd[:, m % 2], fvar[:, m % 2], neghalf[:], ALU.pow).then_inc(f_rstd, 1)

            @block.scalar
            def _(act):
                for n in range(0, NB, SPLIT):
                    act.activation(xhl[:, n:n + SPLIT, 0], xs[:, n:n + SPLIT], ACT.Copy).then_inc(xhi_r, 1)
                act.activation(ident16[:], ident[:], ACT.Copy).then_inc(id16_r, 1)

                def shared_chunk(i, p, h):
                    n = i
                    if live(n, NCH):
                        act.wait_ge(sg_ps, n + 1)
                        wait(act, shid_r, n - 1)
                        act.activation(sgate[:, p], G_BANK[p][:].rearrange("p (m t) -> p m t", m=KT), ACT.Silu).then_inc(sg_r, 1)
                        act.wait_ge(shid_r, n + 1)
                        wait(act, sd_ps, n - 1)
                        act.activation(sh_hi[:, p], shid[:, p], ACT.Copy).then_inc(shhi_r, 1)

                pipeline(act, 2, shared_chunk, NCH)

                def tile(i, s, h):
                    n, q = i - 4, s
                    if live(n, NT):
                        act.wait_ge(eh_r, n + 1)
                        wait(act, dn_ps, n - U + 1)
                        act.activation(eh_hi[:, q], eh[:, q], ACT.Copy).then_inc(ehhi_r, 1)
                    n, q = i - 3, (s - 3) % U
                    if live(n, NT):
                        act.wait_ge(gu_ps, n + 1)
                        wait(act, eh_r, n - U + 1)
                        act.activation(eg[:, q], GU_BANK[q][:, 0:EI], ACT.Silu).then_inc(eg_r, 1)
                    n, q = i - 6, (s - 6) % U
                    if live(n, NT):
                        act.wait_ge(dn_ps, n + 1)
                        wait(act, stored[q], 16 * (h + (s - 6) // U))
                        act.activation(yo[:, q], DN_BANK[q % 2][:, 0:D], ACT.Copy).then_inc(yo_r, 1)

                pipeline(act, LAG3, tile, NT, U)

            @block.vector
            def _(dve):
                def low_part(n):
                    dve.wait_ge(xhi_r, n // SPLIT + 1)
                    dve.tensor_tensor(xhl[:, n:n + SPLIT, 1], xs[:, n:n + SPLIT], xhl[:, n:n + SPLIT, 0], ALU.subtract
                                      ).then_inc(xlo_r, 1)

                low_part(0)
                link = chain(dve, tab_step, TAB_STEPS, 0)
                dve.wait_ge(k_in, 16)
                dve.wait_ge(pads, 2)
                link(dve.tensor_scalar(thr[:], known[:, 1:1 + NB], float(P), None, ALU.mult))
                link(dve.tensor_tensor(over[:], c.count[:].unsqueeze(2).to_broadcast([P, NE, NB]),
                                       thr[:].unsqueeze(1).to_broadcast([P, NE, NB]), ALU.is_gt))
                a, b = 0, 1
                link(dve.tensor_reduce(cums[:, a, PADC:], over[:], AX_X, ALU.add))
                reach = 1
                while reach < NE:
                    link(dve.tensor_tensor(cums[:, b, PADC:], cums[:, a, PADC:], cums[:, a, PADC - reach:PADC + NE - reach], ALU.add))
                    a, b = b, a
                    reach *= 2
                upto = cums[:, a, PADC:]
                before = cums[:, a, PADC - 1:PADC + NE - 1]
                link(dve.tensor_scalar(base[:], before, float(P), 1.0, ALU.mult, ALU.add))
                link(dve.tensor_tensor(ykey[:], c.pos[:], base[:].unsqueeze(1).to_broadcast([P, NB, NE]), ALU.add))
                link(dve.tensor_tensor(ykey[:], ykey[:], c.sel[:], ALU.mult))
                for n in range(NB):
                    dve.max(y8[:, n], ykey[:, n]).then_inc(y8_part, 1)
                dve.wait_ge(y8_part, NB)
                dve.tensor_scalar(y_ix[:], y8[:, :, 0:TOPK], -1.0, None, ALU.add).then_inc(y_ix_ready, 1)
                for n in range(SPLIT, NB, SPLIT):
                    low_part(n)
                dve.wait_ge(xlo_r, NB // SPLIT)
                link(dve.tensor_scalar(after[:], upto, place, None, ALU.is_le))
                link(dve.tensor_reduce(owner[:], after[:], AX_X, ALU.add))
                link(dve.tensor_scalar(owner[:], owner[:], float(NE - 1), None, ALU.min))
                link(dve.tensor_scalar(diag[:], ident[:], owner[:], None, ALU.mult))
                dve.wait_ge(tab_ps, 1)
                dve.tensor_scalar(tile_e[:, EDGE:EDGE + NT], TAB_BANK[:, 0:NT], 0.0, None, ALU.add).then_inc(tab_ready, 1)

                def shared_chunk(i, p, h):
                    n = i
                    if live(n, NCH):
                        dve.wait_ge(sg_r, n + 1)
                        dve.wait_ge(su_ps, n + 1)
                        wait(dve, shlo_r, n - 1)
                        dve.tensor_tensor(shid[:, p], U_BANK[p][:].rearrange("p (m t) -> p m t", m=KT), sgate[:, p], ALU.mult
                                          ).then_inc(shid_r, 1)
                        dve.wait_ge(shhi_r, n + 1)
                        wait(dve, sd_ps, n - 1)
                        dve.tensor_tensor(sh_lo[:, p], shid[:, p], sh_hi[:, p], ALU.subtract).then_inc(shlo_r, 1)
                    n, q = i - 1, 1 - p
                    if live(n, NCH):
                        dve.wait_ge(sd_ps, n + 1)
                        some = bass.ds(n * CT, CT)
                        dve.tensor_tensor(xs[:, some], D_BANK[q][:].rearrange("p (a d) -> p a d", a=CT), xs[:, some], ALU.add
                                          ).then_inc(sacc_r, 1)

                pipeline(dve, 2, shared_chunk, NCH)

                link = chain(dve, weight_step, WEIGHT_STEPS, 0)
                for k in range(TOPK):
                    link(dve.tensor_tensor(same[:], ykey[:], y8[:, :, k:k + 1].to_broadcast([P, NB, NE]), ALU.is_equal))
                    link(dve.tensor_tensor(same[:], same[:], c.wt[:], ALU.mult))
                    link(dve.tensor_reduce(y_w[:, :, k], same[:], AX_X, ALU.add))

                def tile(i, s, h):
                    n, q = i, s
                    if live(n, NT):
                        dve.wait_ge(gt_ps, n + 1)
                        wait(dve, gu_ps, n - U + 1)
                        dve.tensor_copy(gT[:, q], GT_BANK[q % 2]).then_inc(gt_r, 1)
                    n, q = i - 4, s
                    if live(n, NT):
                        dve.wait_ge(ehhi_r, n + 1)
                        dve.tensor_tensor(eh_lo[:, q], eh[:, q], eh_hi[:, q], ALU.subtract).then_inc(ehlo_r, 1)
                    n, q = i - 3, (s - 3) % U
                    if live(n, NT):
                        dve.wait_ge(eg_r, n + 1)
                        wait(dve, ehlo_r, n - U + 1)
                        dve.tensor_tensor(eh[:, q], GU_BANK[q][:, EI:2 * EI], eg[:, q], ALU.mult).then_inc(eh_r, 1)

                pipeline(dve, LAG3, tile, NT, U)

                def final(i, p, h):
                    n = i
                    if live(n):
                        link = chain(dve, ysum_step, SUM_STEPS, n)
                        dve.wait_ge(ygathered[p], 16 * TOPK * (h + 1))
                        wait(dve, fin_r, n - 1)
                        dve.tensor_copy(y_wc[:, p], y_w[:, at(n)].rearrange("p a k -> p (a k)")).then_inc(ywc_r, 1)
                        dve.wait_ge(ywc_r, n + 1)
                        for k in range(TOPK):
                            link(dve.scalar_tensor_tensor(ysum[:, p], yg[:, p, k], y_wc[:, p, k:k + 1],
                                                          ysum[:, p] if k else xs[:, at(n)].rearrange("p a d -> p (a d)"),
                                                          ALU.mult, ALU.add))
                        dve.bn_stats(fstats[:, p], ysum[:, p]).then_inc(f_stat, 1)
                        dve.wait_ge(f_stat, n + 1)
                        settle(dve, n, c.dve_passed, pads, 1)
                        dve.bn_aggr(fmv[:, p], fstats[:, p]).then_inc(f_mv, 1)
                        dve.wait_ge(f_mv, n + 1)
                        wait(dve, f_rstd, n - 1)
                        dve.tensor_scalar(fvar[:, p], fmv[:, p, 1:2], LN_EPS, None, ALU.add).then_inc(f_var, 1)
                    n, q = i - 1, 1 - p
                    if live(n):
                        dve.wait_ge(f_rstd, n + 1)
                        wait(dve, sent[q], 16 * half(h, p, 1))
                        dve.tensor_scalar(fin[:, q], ysum[:, q], fmv[:, q, 0:1], frstd[:, q], ALU.subtract, ALU.mult
                                          ).then_inc(fin_r, 1)

                pipeline(dve, 2, final)

            @block.tensor
            def _(pe):
                def products(o, lhs, rhs, tiles, width):
                    for m in range(tiles):
                        t = 0
                        for x_, y_ in ((0, 0), (0, 1), (1, 0)):
                            for k in range(KT):
                                done = pe.matmul(o[:, m * width:(m + 1) * width], lhs(x_, k, m), rhs(y_, k, m),
                                                 start=t == 0, stop=t == 5)
                                t += 1
                    return done

                def shared_chunk(i, p, h):
                    n = i
                    if live(n, NCH):
                        for col, bank, done in ((C_SG, G_BANK[p], sg_ps), (C_SU, U_BANK[p], su_ps)):
                            wait(pe, shid_r, n - 1)
                            products(bank, lambda s, k, m: W[s][:, k, col + m * P:col + (m + 1) * P],
                                     lambda s, k, m: X[s][:, bass.ds(n * CT, CT), k], KT, CW).then_inc(done, 1)
                    n, q = i - 1, 1 - p
                    if live(n, NCH):
                        H = (sh_hi, sh_lo)
                        pe.wait_ge(shlo_r, n + 1)
                        wait(pe, sacc_r, n - 1)
                        products(D_BANK[q], lambda s, k, m: H[s][:, q, k, m * P:(m + 1) * P],
                                 lambda s, k, m: W[s][:, k, C_SD:C_SD + D], CT, D).then_inc(sd_ps, 1)
                    if isinstance(i, int) and i == 0:
                        pe.wait_ge(tab_step, TAB_STEPS)
                        pe.matmul(TAB_BANK[:, 0:P], c.ones[:], diag[:], start=True, stop=True).then_inc(tab_ps, 1)

                pipeline(pe, 2, shared_chunk, NCH)
                pe.wait_ge(tab_ready, 1)
                pe.wait_ge(id16_r, 1)
                pe.wait_ge(sacc_r, NCH)

                owners = [None] * (LAG3 - 1 + U)

                def tile(i, s, h):
                    if s == 0:
                        _, values = nc.values_load_multi_w_load_instructions(tile_e[0:1, bass.ds(i + EDGE - 5, 5 + U)], engines=[mybir.EngineType.PE],
                                                                    min_val=0, max_val=NE - 1, skip_runtime_bounds_check_because="the table's values are at most NE - 1")
                        owners[:] = values
                    n, q = i - 2, (s - 2) % U
                    if live(n, NT):
                        e = owners[s - 2 + 5]
                        pe.wait_ge(gt_r, n + 1)
                        wait(pe, eh_r, n - U + 1)
                        products(GU_BANK[q], lambda s_, k, m: E[s_][:, at(e), (m * KT + k) * EI:(m * KT + k + 1) * EI].rearrange(
                            "p a w -> p (a w)"), lambda s_, k, m: gT[:, q, s_, k], 2, P).then_inc(gu_ps, 1)
                    n, q = i, s
                    if live(n, NT):
                        pe.wait_ge(gathered[q], 16 * (h + 1))
                        wait(pe, gt_r, n - 1)
                        for part in range(2):
                            for k in range(KT):
                                done = pe.transpose(GT_BANK[q % 2][:, part, k], xg[:, q, part, k], ident16[:])
                        done.then_inc(gt_ps, 1)
                    n, q = i - 5, (s - 5) % U
                    if live(n, NT):
                        e = owners[s - 5 + 5]
                        H = (eh_hi, eh_lo)
                        pe.wait_ge(ehlo_r, n + 1)
                        wait(pe, yo_r, n - 1)
                        for t, (x_, y_) in enumerate(((0, 0), (0, 1), (1, 0))):
                            done = pe.matmul(DN_BANK[q % 2][:, 0:D], H[x_][:, q], E[y_][:, at(e), 4 * EI:6 * EI].rearrange("p a w -> p (a w)"),
                                             start=t == 0, stop=t == 2)
                        done.then_inc(dn_ps, 1)

                pipeline(pe, LAG3, tile, NT, U)


def kernel(**inp):
    import concourse.bacc as bacc
    from concourse.bass_utils import run_bass_kernel_spmd
    a = {k: np.asarray(v) for k, v in inp.items()}
    arrays = host_arrays(a)
    nc = bacc.Bacc("TRN2", target_bir_lowering=False, num_devices=1)
    aps = {n: nc.dram_tensor(f"in_{n}", v.shape, mybir.dt.from_np(v.dtype), kind="ExternalInput").ap() for n, v in arrays.items()}
    out = nc.dram_tensor("out", (NB, P, D), F32, kind="ExternalOutput").ap()
    decoder_kernel(nc, out=out, **aps)
    r = run_bass_kernel_spmd(nc, [{f"in_{n}": v for n, v in arrays.items()}], core_ids=[0])
    return r.results[0]["out"]


def host_arrays(a):
    L, X, F = "L0_attn_", "L0_xattn_", "L0_ffn_"
    wg1 = a[L + "wg1"]
    wcat = np.concatenate(
        [a[L + "wk_lin"], a[L + "wv_lin"], a[L + "wv_loc"], a[L + "wq_lin"], a[L + "wq_loc"], a[L + "wk_loc"],
         wg1[0:D], wg1[D:2 * D], wg1[2 * D:], a[L + "wg2"], a[L + "wo"],
         a[X + "Wq"].T, a[X + "Wk"].T, a[X + "Wv"].T, a[X + "Wo"].T,
         a[F + "shared_gate_w"].T, a[F + "shared_up_w"].T, a[F + "shared_down_w"].T, a[F + "router_weight"].T], axis=1)
    vecs = np.concatenate([a[L + n].reshape(KT, P).T for n in ("ln_g", "ln_b", "bq_lin", "bq_loc", "bk_loc", "bg1", "bg2")], axis=1)
    rowvecs = np.concatenate([a[L + n] for n in ("bk_lin", "bv_lin", "bv_loc", "bo")])
    relpad = np.full((NH, 2 * P - 1), NEG, np.float32)
    relpad[:, P - 1 - HALF:P + HALF] = a[L + "rel_bias"][64 - HALF:64 + HALF + 1].T
    apart = np.arange(P)[None] - np.arange(P)[:, None] + P - 1
    rel = np.stack([relpad[h][apart] for g in range(NG) for h in group_heads(g)], axis=1).reshape(P, NH * P)
    masks = (np.arange(P)[:, None] // HD % 2 == np.arange(2)[None]).astype(np.float32)
    place = np.arange(P, dtype=np.float32)
    eye, earlier = np.eye(P, dtype=np.float32), (place[:, None] < place[None]).astype(np.float32)
    first_row = np.arange(NE, dtype=np.float32) * NB * P
    consts = np.concatenate([eye, earlier, np.tile(first_row + 1, (P, 1)), place[:, None],
                             np.tile(np.arange(NE, dtype=np.float32), (P, 1))], axis=1).astype(np.float32)
    gate, up = (a[F + n].transpose(2, 0, 1).reshape(KT, P, NE, EI).transpose(1, 2, 0, 3).reshape(P, NE, KT * EI) for n in ("gate_w", "up_w"))
    down = a[F + "down_w"].transpose(2, 0, 1)
    experts = np.concatenate([gate, up, down], axis=2)
    ctx_t = a["ctx_1024"].reshape(NB * P, D).T
    return {n: np.ascontiguousarray(v) for n, v in dict(
        x=a["x"], ctx_t=ctx_t, wcat=wcat, vecs=vecs, rowvecs=rowvecs, rel_bias=rel, consts=consts, masks=masks, experts=experts, rbias_d=a[F + "router_bias"]).items()}
```
